# Optimizing a Trainium2 kernel written in Bass

```python
import numpy as np
import jax
import jax.numpy as jnp

def _softmax(x, axis=-1):
    return jax.nn.softmax(x, axis=axis)

def _gelu(x):
    return jax.nn.gelu(x, approximate=True)

def _silu(x):
    return jax.nn.silu(x)

def _sigmoid(x):
    return jax.nn.sigmoid(x)

def _layernorm(x, axis=-1, eps=1e-05):
    m = jnp.mean(x, axis=axis, keepdims=True)
    v = jnp.var(x, axis=axis, keepdims=True)
    return (x - m) / jnp.sqrt(v + eps)

def _scatter_add(tgt, idx, src, axis=0):
    return tgt.at[idx].add(src)

def _segment_sum(src, seg, n):
    return jax.ops.segment_sum(src, seg, n)
kernel_name = 'mk_seq_postln_d2_jaxref_r8_4a9e5d'

def setup_inputs(seed: int=0):
    np.random.seed(seed)
    _w = jnp.asarray

    def _L0_attn_setup():
        import jax, jax.numpy as jnp
        import numpy as np
        import math
        HIDDEN = 128
        key = jax.random.key(seed)
        kx, kq, kk, kv = jax.random.split(key, 4)
        B, S, H = (4, 512, HIDDEN)
        scale = 1.0 / math.sqrt(H)
        x = jax.random.normal(kx, (B, S, H), dtype=jnp.float32)
        Wq = jax.random.normal(kq, (H, H), dtype=jnp.float32) * scale
        Wk = jax.random.normal(kk, (H, H), dtype=jnp.float32) * scale
        Wv = jax.random.normal(kv, (H, H), dtype=jnp.float32) * scale
        return {'x': x, 'Wq': Wq, 'Wk': Wk, 'Wv': Wv}
    _L0_attn_in = _L0_attn_setup()

    def _L0_ffn_setup():
        import jax, jax.numpy as jnp
        import numpy as np
        MIN_EXPERT_CAPACITY = 4
        CAPACITY_FACTOR = 1.0

        def _moe_forward(x, router_w, w1, b1, w2, b2):
            B, S, D = x.shape
            E = router_w.shape[1]
            G = 1
            T = B * S
            C = max(int(round(CAPACITY_FACTOR * T / E)), MIN_EXPERT_CAPACITY)
            xt = x.reshape(G, T, D)
            logits = jnp.einsum('gtd,de->gte', xt, router_w)
            probs = jax.nn.softmax(logits, axis=-1)
            gate = jnp.max(probs, axis=-1)
            idx = jnp.argmax(probs, axis=-1)
            emask = jax.nn.one_hot(idx, E, dtype=x.dtype)
            pos = jnp.cumsum(emask, axis=1) * emask - 1.0
            pos = pos.astype(jnp.int32)
            slot = jax.nn.one_hot(pos, C, dtype=x.dtype)
            dispatch = emask[..., None] * slot
            combine = dispatch * gate[..., None, None]
            expert_inputs = jnp.einsum('gtd,gtec->gecd', xt, dispatch)
            h = jax.nn.relu(jnp.einsum('gecd,edf->gecf', expert_inputs, w1) + b1[None, :, None, :])
            expert_outputs = jnp.einsum('gecf,efd->gecd', h, w2) + b2[None, :, None, :]
            out = jnp.einsum('gecd,gtec->gtd', expert_outputs, combine)
            return out.reshape(B, S, D)
        key = jax.random.key(seed)
        k0, k1, k2, k3 = jax.random.split(key, 4)
        B, S, D, E, F = (4, 256, 128, 8, 512)
        x = jax.random.normal(k0, (B, S, D), dtype=jnp.float32)
        router_w = jax.random.normal(k1, (D, E), dtype=jnp.float32) * D ** (-0.5)
        w1 = jax.random.normal(k2, (E, D, F), dtype=jnp.float32) * D ** (-0.5)
        b1 = jnp.zeros((E, F), dtype=jnp.float32)
        w2 = jax.random.normal(k3, (E, F, D), dtype=jnp.float32) * F ** (-0.5)
        b2 = jnp.zeros((E, D), dtype=jnp.float32)
        return {'x': x, 'router_w': router_w, 'w1': w1, 'b1': b1, 'w2': w2, 'b2': b2}
    _L0_ffn_in = _L0_ffn_setup()

    def _L1_attn_setup():
        import jax, jax.numpy as jnp
        import numpy as np
        B, L, D = (2, 256, 128)
        H, HD = (16, 64)
        LD = 32
        key = jax.random.key(seed)
        ks = jax.random.split(key, 6)
        s = lambda fan_in: 1.0 / np.sqrt(fan_in)
        x_bld = jax.random.normal(ks[0], (B, L, D), dtype=jnp.float32)
        Wq = jax.random.normal(ks[1], (D, H, HD), dtype=jnp.float32) * s(D)
        Wkv_down = jax.random.normal(ks[2], (D, LD), dtype=jnp.float32) * s(D)
        Wk_up = jax.random.normal(ks[3], (LD, H, HD), dtype=jnp.float32) * s(LD)
        Wv_up = jax.random.normal(ks[4], (LD, H, HD), dtype=jnp.float32) * s(LD)
        Wout = jax.random.normal(ks[5], (H, HD, D), dtype=jnp.float32) * s(H * HD)
        return {'x_bld': x_bld, 'Wq': Wq, 'Wkv_down': Wkv_down, 'Wk_up': Wk_up, 'Wv_up': Wv_up, 'Wout': Wout}
    _L1_attn_in = _L1_attn_setup()

    def _L1_ffn_setup():
        import jax, jax.numpy as jnp
        import numpy as np
        B, S, D, H, E = (4, 256, 128, 512, 8)
        key = jax.random.key(seed)
        ks = jax.random.split(key, 8)
        s_d = 1.0 / np.sqrt(D)
        s_h = 1.0 / np.sqrt(H)
        return {'x': jax.random.normal(ks[0], (B, S, D), dtype=jnp.float32), 'gate_w': jax.random.uniform(ks[1], (E, D), jnp.float32, -s_d, s_d), 'gate_b': jax.random.uniform(ks[2], (E,), jnp.float32, -s_d, s_d), 'w1': jax.random.uniform(ks[3], (E, H, D), jnp.float32, -s_d, s_d), 'b1': jax.random.uniform(ks[4], (E, H), jnp.float32, -s_d, s_d), 'w2': jax.random.uniform(ks[5], (E, D, H), jnp.float32, -s_h, s_h), 'b2': jax.random.uniform(ks[6], (E, D), jnp.float32, -s_h, s_h)}
    _L1_ffn_in = _L1_ffn_setup()
    _d = {'L0_attn_x': _L0_attn_in['x'], 'L0_attn_Wq': _L0_attn_in['Wq'], 'L0_attn_Wk': _L0_attn_in['Wk'], 'L0_attn_Wv': _L0_attn_in['Wv'], 'L0_ffn_router_w': _L0_ffn_in['router_w'], 'L0_ffn_w1': _L0_ffn_in['w1'], 'L0_ffn_b1': _L0_ffn_in['b1'], 'L0_ffn_w2': _L0_ffn_in['w2'], 'L0_ffn_b2': _L0_ffn_in['b2'], 'L1_attn_Wq': _L1_attn_in['Wq'], 'L1_attn_Wkv_down': _L1_attn_in['Wkv_down'], 'L1_attn_Wk_up': _L1_attn_in['Wk_up'], 'L1_attn_Wv_up': _L1_attn_in['Wv_up'], 'L1_attn_Wout': _L1_attn_in['Wout'], 'L1_ffn_gate_w': _L1_ffn_in['gate_w'], 'L1_ffn_gate_b': _L1_ffn_in['gate_b'], 'L1_ffn_w1': _L1_ffn_in['w1'], 'L1_ffn_b1': _L1_ffn_in['b1'], 'L1_ffn_w2': _L1_ffn_in['w2'], 'L1_ffn_b2': _L1_ffn_in['b2']}
    _x0 = _d['L0_attn_x']
    _d['L0_attn_x'] = jax.random.normal(jax.random.fold_in(jax.random.key(seed), 1), (2, 1024, 128), dtype=_x0.dtype)
    del _x0
    return _d

def reference(L0_attn_x, L0_attn_Wq, L0_attn_Wk, L0_attn_Wv, L0_ffn_router_w, L0_ffn_w1, L0_ffn_b1, L0_ffn_w2, L0_ffn_b2, L1_attn_Wq, L1_attn_Wkv_down, L1_attn_Wk_up, L1_attn_Wv_up, L1_attn_Wout, L1_ffn_gate_w, L1_ffn_gate_b, L1_ffn_w1, L1_ffn_b1, L1_ffn_w2, L1_ffn_b2):

    def _L0_attn_ref(x, Wq, Wk, Wv):
        import jax, jax.numpy as jnp
        import numpy as np
        import math
        HIDDEN = 128
        B, S, H = x.shape
        q = jnp.einsum('bsh,oh->bso', x, Wq)
        k = jnp.einsum('bsh,oh->bso', x, Wk)
        v = jnp.einsum('bsh,oh->bso', x, Wv)
        scores = jnp.einsum('bqh,bkh->bqk', q, k) / jnp.sqrt(jnp.float32(H))
        causal = jnp.tril(jnp.ones((S, S), dtype=bool))
        scores = jnp.where(causal[None, :, :], scores, -jnp.inf)
        att = jax.nn.softmax(scores, axis=-1)
        return jnp.einsum('bqk,bkh->bqh', att, v)

    def _L0_ffn_ref(x, router_w, w1, b1, w2, b2):
        import jax, jax.numpy as jnp
        import numpy as np
        MIN_EXPERT_CAPACITY = 4
        CAPACITY_FACTOR = 1.0

        def _moe_forward(x, router_w, w1, b1, w2, b2):
            B, S, D = x.shape
            E = router_w.shape[1]
            G = 1
            T = B * S
            C = max(int(round(CAPACITY_FACTOR * T / E)), MIN_EXPERT_CAPACITY)
            xt = x.reshape(G, T, D)
            logits = jnp.einsum('gtd,de->gte', xt, router_w)
            probs = jax.nn.softmax(logits, axis=-1)
            gate = jnp.max(probs, axis=-1)
            idx = jnp.argmax(probs, axis=-1)
            emask = jax.nn.one_hot(idx, E, dtype=x.dtype)
            pos = jnp.cumsum(emask, axis=1) * emask - 1.0
            pos = pos.astype(jnp.int32)
            slot = jax.nn.one_hot(pos, C, dtype=x.dtype)
            dispatch = emask[..., None] * slot
            combine = dispatch * gate[..., None, None]
            expert_inputs = jnp.einsum('gtd,gtec->gecd', xt, dispatch)
            h = jax.nn.relu(jnp.einsum('gecd,edf->gecf', expert_inputs, w1) + b1[None, :, None, :])
            expert_outputs = jnp.einsum('gecf,efd->gecd', h, w2) + b2[None, :, None, :]
            out = jnp.einsum('gecd,gtec->gtd', expert_outputs, combine)
            return out.reshape(B, S, D)
        return _moe_forward(x, router_w, w1, b1, w2, b2)

    def _L1_attn_ref(x_bld, Wq, Wkv_down, Wk_up, Wv_up, Wout):
        import jax, jax.numpy as jnp
        import numpy as np
        B, L, D = (2, 256, 128)
        H, HD = (16, 64)
        LD = 32
        q_blhd = jnp.einsum('bld,dhk->blhk', x_bld, Wq)
        latent_bll = jnp.einsum('bld,dc->blc', x_bld, Wkv_down)
        k_blhd = jnp.einsum('blc,chk->blhk', latent_bll, Wk_up)
        v_blhd = jnp.einsum('blc,chk->blhk', latent_bll, Wv_up)
        attn = jnp.einsum('bqhd,bkhd->bhqk', q_blhd, k_blhd) / jnp.sqrt(jnp.asarray(HD, dtype=x_bld.dtype))
        l = x_bld.shape[1]
        mask = (jnp.arange(l)[None, :] <= jnp.arange(l)[:, None])[None, None]
        neg_inf = jnp.finfo(attn.dtype).min
        attn = jax.nn.softmax(jnp.where(mask, attn, neg_inf), axis=-1)
        y_blhd = jnp.einsum('bhqk,bkhd->bqhd', attn, v_blhd)
        return jnp.einsum('bqhd,hdo->bqo', y_blhd, Wout)

    def _L1_ffn_ref(x, gate_w, gate_b, w1, b1, w2, b2):
        import jax, jax.numpy as jnp
        import numpy as np
        B, S, D, H, E = (4, 256, 128, 512, 8)
        b, s, d = x.shape
        xf = x.reshape(-1, d)
        logits = xf @ gate_w.T + gate_b
        top1 = jnp.argmax(logits, axis=-1)
        out = jnp.zeros_like(xf)
        n_experts = w1.shape[0]
        for e in range(n_experts):
            h = jax.nn.relu(xf @ w1[e].T + b1[e])
            y = h @ w2[e].T + b2[e]
            out = out + jnp.where((top1 == e)[:, None], y, jnp.zeros((), y.dtype))
        return out.reshape(b, s, d)
    x = L0_attn_x
    x = _layernorm(x + _L0_attn_ref(x, L0_attn_Wq, L0_attn_Wk, L0_attn_Wv), axis=-1)
    x = _layernorm(x + _L0_ffn_ref(x, L0_ffn_router_w, L0_ffn_w1, L0_ffn_b1, L0_ffn_w2, L0_ffn_b2), axis=-1)
    x = _layernorm(x + _L1_attn_ref(x, L1_attn_Wq, L1_attn_Wkv_down, L1_attn_Wk_up, L1_attn_Wv_up, L1_attn_Wout), axis=-1)
    x = _layernorm(x + _L1_ffn_ref(x, L1_ffn_gate_w, L1_ffn_gate_b, L1_ffn_w1, L1_ffn_b1, L1_ffn_w2, L1_ffn_b2), axis=-1)
    return x

_drawn_inputs = setup_inputs


def setup_inputs(seed=0):
    import zlib

    import numpy as np

    out = dict(_drawn_inputs(seed))
    spreads = {'L0_ffn_b1': (0.0, 0.1), 'L0_ffn_b2': (0.0, 0.1)}
    factors = {'L1_ffn_b1': 2.847}
    for name, (base, spread) in spreads.items():
        noise = np.random.default_rng([zlib.crc32(name.encode()), seed]).standard_normal(out[name].shape)
        drawn = base * np.exp(spread * noise) if base else spread * noise
        out[name] = jnp.asarray(drawn.astype(out[name].dtype))
    for name, factor in factors.items():
        out[name] = (out[name] * factor).astype(out[name].dtype)
    return out
```

```python
from contextlib import ExitStack

import concourse.bass as bass
from concourse import mybir

ALU = mybir.AluOpType
ACT = mybir.ActivationFunctionType
AX = mybir.AxisListType
F32 = mybir.dt.float32
F16 = mybir.dt.float16
BF16 = mybir.dt.bfloat16
I32 = mybir.dt.int32

P = 128
D = 128
EPS = 1e-5
NEG = -1e38
KB = 4


class Chain:

    def __init__(self, eng, sem):
        self.eng, self.sem, self.n = eng, sem, 0

    def step(self, ins):
        self.n += 1
        ins.then_inc(self.sem, 1)
        self.eng.wait_ge(self.sem, self.n)


def build(nc, x_tok_d, x_t_d, wq0, wk0, wv0_t, router, w1a_d, b1a_d, w2a_d, b2a_d,
          wq1_t, wkv, wku_t, wvu_t, wout, gate_w_t, gate_b, w1b_d, b1b_d, w2b_d, b2b_d,
          const_f_d, const_b_d, out_d):
    T = x_tok_d.shape[0]
    B = 2
    S = T // B
    NT = T // P
    NS = S // P
    E = router.shape[1]
    F = w1a_d.shape[2]
    FC = F // P
    W1 = F + FC
    H, HD, LD = wq1_t.shape[1], wq1_t.shape[0], wkv.shape[1]
    G = H * LD // P
    HG = H // G
    CAP = max(round(T / E), 4)
    TILES = (E * CAP // P, NT + E - 1)
    SCALE0, SCALE1 = float(D) ** -0.5, float(HD) ** -0.5

    ctx = ExitStack()
    with ctx:
        def sb(name, shape, dt=F32):
            return ctx.enter_context(nc.sbuf_tensor(name, shape, dt))

        def sem(name):
            return ctx.enter_context(nc.semaphore(name))

        x0 = sb("x0", [P, NT, D])
        xt = sb("xt", [P, T])
        pre = sb("pre", [P, NT, D])
        xa = sb("xa", [P, NT, D])
        xb = sb("xb", [P, NT, D])
        got = x0
        stats = sb("stats", [P, NT, 6])
        mv = sb("mv", [P, NT, 2])
        var = sb("var", [P, NT])
        rstd = sb("rstd", [P, NT])

        cf = sb("cf", [P, 4 * P + NT * E + E * NT + 32])
        ident = cf[:, 0:P]
        rank = cf[:, P:P + NT * E].rearrange("p (t e) -> p t e", e=E)
        edge = cf[:, 2 * P:2 * P + E * NT].rearrange("p (e j) -> p e j", j=NT)
        tile_no = cf[:, 3 * P:3 * P + TILES[1] * E].rearrange("p (t e) -> p t e", e=E)
        half = cf[:, 3 * P + TILES[1] * E:3 * P + TILES[1] * E + NT]
        cb = sb("cb", [P, 5 * P], BF16)
        ident_b, ones_b, upper_b = (cb[:, i * P:(i + 1) * P] for i in range(3))
        mask_qk, mask_kq = (cb[:, i * P:(i + 1) * P] for i in range(3, 5))
        ones_f = sb("ones_f", [1, P])

        w1 = sb("w1", [P, E, W1])
        w2 = sb("w2", [P, E, FC, D])
        b2 = sb("b2", [1, E, D])
        rt = sb("rt", [P, 2, E])
        gb = sb("gb", [1, E])
        wsm = sb("wsm", [P, 3, P])
        wkv_s = sb("wkv_s", [P, 4, LD])
        wqk = sb("wqk", [P, H * LD])
        wvo = sb("wvo", [P, G, D])

        psum = ctx.enter_context(nc.psum_tensor("psum", [P, 8, 512], F32))

        slots_d = [nc.dram_tensor(f"slots{i}", [TILES[i] * P, D], F32, kind="Internal").ap() for i in range(2)]
        outs_d = [nc.dram_tensor(f"outs{i}", [TILES[i] * P, D], F32, kind="Internal").ap() for i in range(2)]
        q_d = nc.dram_tensor("q_parts", [2, H * LD, T], F16, kind="Internal").ap()

        s_small = sem("small_weights_in")
        s_x = sem("x_in")
        s_w = [sem("experts0_in"), sem("experts1_in")]
        s_heads = sem("head_weights_in")
        s_zero = sem("scratch_zeroed")

        def load_experts(eng, layer):
            w1_d, b1_d, w2_d, b2_d = ((w1a_d, b1a_d, w2a_d, b2a_d), (w1b_d, b1b_d, w2b_d, b2b_d))[layer]
            eng.dma_start(w1[:, :, 0:F], w1_d.rearrange("e d f -> d e f")).then_inc(s_w[layer], 16)
            eng.dma_start(w1[:, :, F:W1], b1_d.rearrange("p (e c) -> p e c", c=FC)).then_inc(s_w[layer], 16)
            for e in range(E):
                eng.dma_start(w2[:, e], w2_d[e].rearrange("(c p) d -> p c d", p=P)).then_inc(s_w[layer], 16)
            eng.dma_start(b2[:], b2_d.rearrange("(o e) d -> o e d", o=1)).then_inc(s_w[layer], 16)

        EXPERT_LOADS = 16 * (3 + E)

        def norm_stats(dve, ch, t):
            ch.step(dve.bn_stats(stats[:, t, :], pre[:, t, :]))
            return dve.bn_aggr(mv[:, t, :], stats[:, t, :])

        def norm_rstd(pool, s_stats, s_var, s_rstd):
            pool.wait_ge(s_stats, NT)
            pool.tensor_scalar(var[:], mv[:, :, 1], EPS, None, ALU.add).then_inc(s_var, 1)
            pool.wait_ge(s_var, 1)
            pool.tensor_tensor(rstd[:], var[:], half, ALU.pow).then_inc(s_rstd, 1)

        def norm_apply(dve, dst, s_rstd, s_norm):
            dve.wait_ge(s_rstd, 1)
            for t in range(NT):
                dve.tensor_scalar(dst[:, t, :], pre[:, t, :], mv[:, t, 0:1], rstd[:, t:t + 1],
                                  ALU.subtract, ALU.mult).then_inc(s_norm, 1)

        def attend0():
            c2 = ExitStack()
            with c2, nc.Block() as block:
                def sb2(name, shape, dt=F32):
                    return c2.enter_context(nc.sbuf_tensor(name, shape, dt))

                qk = sb2("qk", [P, P])
                qt = sb2("qt", [P, T])
                v = sb2("v", [P, NT, D])
                prob = sb2("prob", [P, 2, S])
                prob_t = sb2("prob_t", [P, 2, NS, P])
                m = sb2("m", [P, NT])
                nm = sb2("nm", [P, NT])
                den = sb2("den", [P, NT])
                rden = sb2("rden", [P, NT])
                hw = sb2("hw", [HD, H, P + 2 * LD + D])
                zeros = sb2("zeros", [P, 512])
                cb_f = sb2("cb_f", [P, 5 * P])
                s_qk, s_qkc, s_qt, s_qtc, s_v, s_vc = (sem("a0_" + n) for n in
                                                       ("qk", "qk_copied", "q", "q_copied", "v", "v_copied"))
                s_sc, s_m, s_nm, s_exp, s_tr, s_trc, s_o, s_oc = (sem("a0_" + n) for n in (
                    "scored", "max", "neg_max", "exp", "turned", "turned_copied", "out", "out_taken"))
                s_ch, s_stats, s_var, s_rstd, s_norm = (sem("a0_" + n) for n in
                                                        ("dve_chain", "stats", "var", "rstd", "normed"))
                s_hw, s_hwc, s_z, s_ones, s_cb_in, s_cb = (sem("a0_" + n) for n in (
                    "head_w", "head_w_copied", "zeros", "ones", "masks_in", "masks"))
                first = [sum((r % NS) // KB + 1 for r in range(i)) for i in range(NT + 1)]

                @block.sync
                def _(sp):
                    sp.dma_start(wsm[:, 0, :], wq0).then_inc(s_small, 16)
                    sp.dma_start(wsm[:, 1, :], wk0).then_inc(s_small, 16)
                    sp.dma_start(xt[:], x_t_d).then_inc(s_x, 16)
                    sp.dma_start(wsm[:, 2, :], wv0_t).then_inc(s_small, 16)
                    sp.dma_start(cb_f[:], const_b_d).then_inc(s_cb_in, 16)
                    sp.dma_start(cf[:], const_f_d).then_inc(s_small, 16)
                    sp.dma_start(x0[:], x_tok_d.rearrange("(t p) d -> p t d", p=P)).then_inc(s_x, 16)
                    sp.dma_start(rt[:, 0, :], router).then_inc(s_small, 16)
                    sp.dma_start(rt[:, 1, :], gate_w_t).then_inc(s_small, 16)
                    sp.dma_start(gb[:], gate_b.rearrange("(o e) -> o e", o=1)).then_inc(s_small, 16)
                    for r in range(4):
                        sp.dma_start(wkv_s[:, r, :], wkv).then_inc(s_small, 16)
                    sp.dma_start(hw[:, :, 0:P], wq1_t).then_inc(s_heads, 16)
                    sp.dma_start(hw[:, :, P:P + LD], wku_t).then_inc(s_heads, 16)
                    sp.dma_start(hw[:, :, P + LD:P + 2 * LD], wvu_t).then_inc(s_heads, 16)
                    sp.dma_start(hw[:, :, P + 2 * LD:], wout).then_inc(s_heads, 16)
                    load_experts(sp, 0)
                    sp.wait_ge(s_z, 1)
                    for layer in range(2):
                        rows = slots_d[layer].rearrange("(n p) d -> p n d", p=P)
                        for n in range(0, TILES[layer], 4):
                            k = min(4, TILES[layer] - n)
                            sp.dma_start(rows[:, n:n + k, :], zeros[:, 0:k * D].rearrange("p (n d) -> p n d", d=D)
                                         ).then_inc(s_zero, 16)
                    sp.wait_ge(s_zero, 16 * sum(-(-n // 4) for n in TILES))
                    sp.wait_ge(s_heads, 64)

                @block.gpsimd
                def _(pool):
                    pool.memset(zeros[:], 0.0).then_inc(s_z, 1)
                    pool.memset(ones_f[:], 1.0).then_inc(s_ones, 1)
                    pool.wait_ge(s_cb_in, 16)
                    pool.tensor_copy(cb[:], cb_f[:]).then_inc(s_cb, 1)
                    norm_rstd(pool, s_stats, s_var, s_rstd)

                @block.tensor
                def _(pe):
                    pe.wait_ge(s_small, 16 * 11)
                    pe.matmul(psum[:, 7, 0:P], wsm[:, 0, :], wsm[:, 1, :], start=True, stop=True).then_inc(s_qk, 1)
                    pe.wait_ge(s_x, 32)
                    for t in range(NT):
                        mm = pe.matmul(psum[:, t // KB, (t % KB) * D:(t % KB + 1) * D], xt[:, t * P:(t + 1) * P],
                                       wsm[:, 2, :], start=True, stop=True)
                        if t % KB == KB - 1:
                            mm.then_inc(s_v, 1)
                    pe.wait_ge(s_qkc, 1)
                    for c in range(T // 512):
                        pe.matmul(psum[:, 4 + c, :], qk[:], xt[:, c * 512:(c + 1) * 512],
                                  start=True, stop=True).then_inc(s_qt, 1)

                    def scores(i):
                        b, r = divmod(i, NS)
                        if i == 0:
                            pe.wait_ge(s_qtc, T // 512)
                            pe.wait_ge(s_vc, T // 512)
                            pe.wait_ge(s_cb, 1)
                        if i >= 2:
                            pe.wait_ge(s_exp, i - 1)
                        w = (r + 1) * P
                        for c in range(0, w, 512):
                            k = min(512, w - c)
                            last = c + k == w
                            dst = psum[:, 2 * (i % 2) + c // 512, 0:k]
                            pe.matmul(dst, qt[:, i * P:(i + 1) * P], xt[:, b * S + c:b * S + c + k],
                                      start=True, stop=not last)
                        pe.matmul(dst[:, k - P:k], ident_b, mask_qk, start=False, stop=True).then_inc(s_sc, 1)

                    def turn(i):
                        r = i % NS
                        pe.wait_ge(s_exp, i + 1)
                        for c in range(r // KB + 1):
                            n = first[i] + c
                            if n >= 2:
                                pe.wait_ge(s_trc, n - 1)
                            for j in range(c * KB, min(r + 1, (c + 1) * KB)):
                                mm = pe.transpose(psum[:, 4 + n % 2, (j % KB) * P:(j % KB + 1) * P],
                                                  prob[:, i % 2, j * P:(j + 1) * P], ident)
                            mm.then_inc(s_tr, 1)

                    def weigh(i):
                        b, r = divmod(i, NS)
                        pe.wait_ge(s_trc, first[i + 1])
                        if i >= 2:
                            pe.wait_ge(s_oc, i - 1)
                        for j in range(r + 1):
                            mm = pe.matmul(psum[:, 6 + i % 2, 0:D], prob_t[:, i % 2, j, :], v[:, b * NS + j, :],
                                           start=(j == 0), stop=(j == r))
                        mm.then_inc(s_o, 1)

                    scores(0)
                    for i in range(NT):
                        if i + 1 < NT:
                            scores(i + 1)
                        turn(i)
                        weigh(i)
                    pe.wait_ge(s_heads, 64)
                    pe.wait_ge(s_exp, NT)
                    for h in range(H):
                        mm = pe.matmul(psum[:, 0, h * LD:(h + 1) * LD], hw[:, h, 0:P], hw[:, h, P:P + LD],
                                       start=True, stop=True)
                    mm.then_inc(s_hw, 1)
                    for h in range(H):
                        o = (h % HG) * LD
                        mm = pe.matmul(psum[o:o + LD, 1, (h // HG) * D:(h // HG + 1) * D],
                                       hw[:, h, P + LD:P + 2 * LD], hw[:, h, P + 2 * LD:], start=True, stop=True)
                    mm.then_inc(s_hw, 1)

                @block.scalar
                def _(act):
                    for c in range(T // 512):
                        act.wait_ge(s_v, c + 1)
                        nc.scalar.copy(v[:, c * KB:(c + 1) * KB, :],
                                       psum[:, c, :].rearrange("p (t d) -> p t d", d=D)).then_inc(s_vc, 1)
                    for i in range(NT):
                        w = (i % NS + 1) * P
                        act.wait_ge(s_nm, i + 1)
                        if i >= 2:
                            act.wait_ge(s_tr, first[i - 1])
                        nc.scalar.activation(prob[:, i % 2, 0:w],
                                             psum[:, 2 * (i % 2):2 * (i % 2) + 2, :].rearrange("p a n -> p (a n)")[:, 0:w],
                                             ACT.Exp, bias=nm[:, i:i + 1], scale=SCALE0,
                                             accum_out=den[:, i:i + 1]).then_inc(s_exp, 1)
                    act.wait_ge(s_hw, 1)
                    nc.scalar.copy(wqk[:], psum[:, 0, :]).then_inc(s_hwc, 1)
                    act.wait_ge(s_hw, 2)
                    nc.scalar.copy(wvo[:], psum[:, 1, :].rearrange("p (g d) -> p g d", d=D)).then_inc(s_hwc, 1)

                @block.vector
                def _(dve):
                    ch = Chain(dve, s_ch)
                    dve.wait_ge(s_qk, 1)
                    dve.tensor_copy(qk[:], psum[:, 7, 0:P]).then_inc(s_qkc, 1)
                    for c in range(T // 512):
                        dve.wait_ge(s_qt, c + 1)
                        dve.tensor_copy(qt[:, c * 512:(c + 1) * 512], psum[:, 4 + c, :]).then_inc(s_qtc, 1)

                    def row_max(i):
                        w = (i % NS + 1) * P
                        dve.wait_ge(s_sc, i + 1)
                        dve.tensor_reduce(m[:, i:i + 1], psum[:, 2 * (i % 2):2 * (i % 2) + 2, :].rearrange(
                            "p a n -> p (a n)")[:, 0:w], AX.X, ALU.max).then_inc(s_m, 1)
                        dve.wait_ge(s_m, i + 1)
                        dve.tensor_scalar(nm[:, i:i + 1], m[:, i:i + 1], -SCALE0, None, ALU.mult).then_inc(s_nm, 1)

                    row_max(0)
                    for i in range(NT):
                        if i + 1 < NT:
                            row_max(i + 1)
                        r = i % NS
                        for c in range(r // KB + 1):
                            n = first[i] + c
                            k = min(KB, r + 1 - c * KB)
                            dve.wait_ge(s_tr, n + 1)
                            if i >= 2 and c == 0:
                                dve.wait_ge(s_o, i - 1)
                            dve.tensor_copy(prob_t[:, i % 2, c * KB:c * KB + k, :],
                                            psum[:, 4 + n % 2, 0:k * P].rearrange("p (j q) -> p j q", q=P)
                                            ).then_inc(s_trc, 1)
                        dve.wait_ge(s_exp, i + 1)
                        ch.step(dve.reciprocal(rden[:, i:i + 1], den[:, i:i + 1]))
                        dve.wait_ge(s_o, i + 1)
                        ins = dve.scalar_tensor_tensor(pre[:, i, :], psum[:, 6 + i % 2, 0:D], rden[:, i:i + 1],
                                                       x0[:, i, :], ALU.mult, ALU.add)
                        ins.then_inc(s_oc, 1)
                        dve.wait_ge(s_oc, i + 1)
                        norm_stats(dve, ch, i).then_inc(s_stats, 1)
                    norm_apply(dve, xa, s_rstd, s_norm)

        def experts(layer, src, dst):
            tiles = TILES[layer]
            c2 = ExitStack()
            with c2:
                def sb2(name, shape, dt=F32):
                    return c2.enter_context(nc.sbuf_tensor(f"f{layer}_{name}", shape, dt))

                def sm(name):
                    return sem(f"f{layer}_{name}")

                slot = sb2("slot", [P, NT], I32)
                owner = sb2("owner", [1, tiles], I32)
                gate = sb2("gate", [P, NT])

                with ExitStack() as c3, nc.Block() as block:
                    def sb3(name, shape, dt=F32):
                        return c3.enter_context(nc.sbuf_tensor(f"f{layer}_{name}", shape, dt))

                    top = sb3("top", [P, NT])
                    lg = sb3("lg", [P, NT, E])
                    hit = sb3("hit", [P, NT, E])
                    cand = sb3("cand", [P, NT, E])
                    best = sb3("best", [P, NT])
                    pick = sb3("pick", [P, NT, E])
                    pick_b = sb3("pick_b", [P, NT * E], BF16)
                    ex = sb3("ex", [P, NT, E])
                    cnt = sb3("cnt", [P, NT, E])
                    count = sb3("count", [P, NT])
                    place = sb3("place", [P, NT])
                    over = sb3("over", [P, NT])
                    den = sb3("den", [P, NT])
                    tot = sb3("tot", [P, E])
                    more = sb3("more", [P, E, NT])
                    used = sb3("used", [P, E])
                    ends = sb3("ends", [P, 2, E])
                    offs = sb3("offs", [P, E])
                    past = sb3("past", [1, tiles, E])
                    own_f = sb3("own_f", [1, tiles])
                    s_tr, s_trc, s_lg, s_ch, s_pick, s_cnt, s_dif, s_ex, s_slot, s_sc = (sm(n) for n in (
                        "turned", "turned_copied", "logits", "route_chain", "picked", "counted", "dif", "exp",
                        "slots", "scattered"))

                    @block.tensor
                    def _(pe):
                        for c in range(NT // KB):
                            for t in range(c * KB, (c + 1) * KB):
                                mm = pe.transpose(psum[:, c, (t % KB) * P:(t % KB + 1) * P], src[:, t, :], ident)
                            mm.then_inc(s_tr, 1)
                        for t in range(NT):
                            if t % KB == 0:
                                pe.wait_ge(s_trc, t // KB + 1)
                            dst_l = psum[:, 4, t * E:(t + 1) * E]
                            mm = pe.matmul(dst_l, xt[:, t * P:(t + 1) * P], rt[:, layer, :],
                                           start=True, stop=(layer == 0))
                            if layer == 1:
                                mm = pe.matmul(dst_l, ones_f[:], gb[:], start=False, stop=True)
                        mm.then_inc(s_lg, 1)
                        pe.wait_ge(s_pick, 1)
                        pe.matmul(psum[:, 5, 0:NT * E], upper_b, pick_b[:], start=True, stop=False)
                        for s in range(1, NT):
                            mm = pe.matmul(psum[:, 5, s * E:NT * E], ones_b, pick_b[:, 0:(NT - s) * E],
                                           start=False, stop=(s == NT - 1))
                        mm.then_inc(s_cnt, 1)
                        for t in range(NT):
                            mm = pe.matmul(psum[:, 6, 0:E], ones_b, pick_b[:, t * E:(t + 1) * E],
                                           start=(t == 0), stop=(t == NT - 1))
                        mm.then_inc(s_cnt, 1)

                    @block.scalar
                    def _(act):
                        for c in range(NT // KB):
                            act.wait_ge(s_tr, c + 1)
                            nc.scalar.copy(xt[:, c * 512:(c + 1) * 512], psum[:, c, :]).then_inc(s_trc, 1)
                        if layer == 0:
                            act.wait_ge(s_dif, 1)
                            nc.scalar.activation(ex[:], ex[:], ACT.Exp).then_inc(s_ex, 1)

                    @block.vector
                    def _(dve):
                        ch = Chain(dve, s_ch)

                        def wide(a):
                            return a.unsqueeze(2).broadcast_to((P, NT, E))

                        dve.wait_ge(s_lg, 1)
                        ch.step(dve.tensor_copy(lg[:], psum[:, 4, 0:NT * E].rearrange("p (t e) -> p t e", e=E)))
                        ch.step(dve.tensor_reduce(top[:], lg[:], AX.X, ALU.max))
                        ch.step(dve.tensor_tensor(hit[:], lg[:], wide(top[:]), ALU.is_equal))
                        ch.step(dve.tensor_tensor(cand[:], hit[:], rank, ALU.mult))
                        ch.step(dve.tensor_reduce(best[:], cand[:], AX.X, ALU.max))
                        ch.step(dve.tensor_tensor(pick[:], rank, wide(best[:]), ALU.is_equal))
                        dve.tensor_copy(pick_b[:], pick[:].rearrange("p t e -> p (t e)")).then_inc(s_pick, 1)
                        if layer == 0:
                            dve.tensor_tensor(ex[:], lg[:], wide(top[:]), ALU.subtract).then_inc(s_dif, 1)
                            dve.wait_ge(s_ex, 1)
                            ch.step(dve.tensor_reduce(den[:], ex[:], AX.X, ALU.add))
                            ch.step(dve.reciprocal(gate[:], den[:]))
                        dve.wait_ge(s_cnt, 1)
                        counted = psum[:, 5, 0:NT * E].rearrange("p (t e) -> p t e", e=E)
                        if layer == 0:
                            ch.step(dve.tensor_tensor(cnt[:], counted, pick[:], ALU.mult))
                            ch.step(dve.tensor_reduce(count[:], cnt[:], AX.X, ALU.add))
                            ch.step(dve.tensor_scalar(place[:], best[:], -float(CAP), float(CAP * E - 1),
                                                      ALU.mult, ALU.add))
                            ch.step(dve.tensor_tensor(place[:], place[:], count[:], ALU.add))
                            ch.step(dve.tensor_scalar(over[:], count[:], float(CAP), float(CAP * E), ALU.is_gt, ALU.mult))
                            ch.step(dve.tensor_tensor(place[:], place[:], over[:], ALU.add))
                        else:
                            dve.wait_ge(s_cnt, 2)
                            ch.step(dve.tensor_copy(tot[:], psum[:, 6, 0:E]))
                            ch.step(dve.tensor_tensor(more[:], tot[:].unsqueeze(2).broadcast_to((P, E, NT)), edge,
                                                      ALU.is_gt))
                            ch.step(dve.tensor_reduce(used[:], more[:], AX.X, ALU.add))
                            ch.step(dve.tensor_copy(ends[:, 0, :], used[:]))
                            k, at = 1, 0
                            while k < E:
                                ch.step(dve.tensor_copy(ends[:, 1 - at, 0:k], ends[:, at, 0:k]))
                                ch.step(dve.tensor_tensor(ends[:, 1 - at, k:E], ends[:, at, k:E], ends[:, at, 0:E - k],
                                                          ALU.add))
                                k, at = 2 * k, 1 - at
                            ch.step(dve.tensor_tensor(offs[:], ends[:, at, :], used[:], ALU.subtract))
                            ch.step(dve.tensor_scalar(offs[:], offs[:], float(P), -1.0, ALU.mult, ALU.add))
                            ch.step(dve.tensor_tensor(cnt[:], counted, offs[:].unsqueeze(1).broadcast_to((P, NT, E)),
                                                      ALU.add))
                            ch.step(dve.tensor_tensor(cnt[:], cnt[:], pick[:], ALU.mult))
                            ch.step(dve.tensor_reduce(place[:], cnt[:], AX.X, ALU.add))
                            ch.step(dve.tensor_tensor(past[:], ends[0:1, at, :].unsqueeze(1).broadcast_to((1, tiles, E)),
                                                      tile_no[0:1, 0:tiles, :], ALU.is_le))
                            ch.step(dve.tensor_reduce(own_f[:], past[:], AX.X, ALU.add))
                            ch.step(dve.tensor_scalar(own_f[:], own_f[:], float(E - 1), None, ALU.min))
                            ch.step(dve.tensor_copy(owner[:], own_f[:]))
                        dve.tensor_copy(slot[:], place[:]).then_inc(s_slot, 1)

                    @block.gpsimd
                    def _(pool):
                        pool.wait_ge(s_slot, 1)
                        for t in range(NT):
                            pool.indirect_dma_start(
                                slots_d[layer], bass.IndirectOffsetOnAxis(ap=slot[:, t:t + 1], axis=0),
                                src[:, t, :], None, bounds_check=tiles * P - 1, oob_is_err=False).then_inc(s_sc, 16)
                        pool.wait_ge(s_sc, 16 * NT)

                with ExitStack() as c3, nc.Block() as block:
                    def sb3(name, shape, dt=F32):
                        return c3.enter_context(nc.sbuf_tensor(f"f{layer}_{name}", shape, dt))

                    rows = sb3("rows", [P, 2, D])
                    rows_t = sb3("rows_t", [P, 2, P])
                    w1_now = sb3("w1_now", [P, 2, W1])
                    hid = sb3("hid", [P, 2, FC, P])
                    ybuf = sb3("ybuf", [P, 2, D])
                    s_in = [sm("rows_in_a"), sm("rows_in_b")]
                    s_out = [sm("out_stored_a"), sm("out_stored_b")]
                    s_tr, s_trc, s_w1, s_h, s_ra, s_rb, s_y, s_yc = (sm(n) for n in (
                        "row_turned", "row_copied", "w1_chosen", "hidden", "relu_act", "relu_dve", "out", "out_copied"))
                    loops = (tiles - 3) // 2
                    begin, end = 2, 2 + 2 * ((tiles - 4) // 2)

                    def expert_of(eng, t, k=None, off=0):
                        if layer == 0:
                            return t * P // CAP if k is None else k + (off * P) // CAP
                        if k is None:
                            return eng.value_load(owner[0:1, t:t + 1], min_val=0, max_val=E - 1)
                        return eng.value_load(owner[0:1, bass.ds(2 * k + off, 1)], min_val=0, max_val=E - 1)

                    def over_tiles(eng, body, start, stop):
                        lo = start + 4 + start % 2
                        hi = lo + 2 * ((stop - 2 - lo) // 2)
                        for t in range(start, lo):
                            body(t, t % 2, None, 0)
                        with eng.Fori(lo // 2, hi // 2) as k:
                            body(2 * k, 0, k, 0)
                            body(2 * k + 1, 1, k, 1)
                        for t in range(hi, stop):
                            body(t, t % 2, None, 0)

                    @block.sync
                    def _(sp):
                        def load(t, par, k, off):
                            if k is not None or t >= 2:
                                sp.wait_ge(s_tr, t - 1)
                            sp.dma_start(rows[:, par, :], slots_d[layer][bass.ds(t * P, P), :]).then_inc(s_in[par], 16)
                        over_tiles(sp, load, 0, tiles)

                    @block.tensor
                    def _(pe):
                        pe.wait_ge(s_w[layer], EXPERT_LOADS)

                        def turn(t, par, k, off):
                            pe.wait_ge(s_in[par], 16 * (k + (off // 2) + 1) if k is not None else 16 * (t // 2 + 1))
                            if k is not None or t >= 2:
                                pe.wait_ge(s_trc, t - 1)
                            pe.transpose(psum[:, par, 0:P], rows[:, par, :], ident).then_inc(s_tr, 1)

                        def hidden(t, par, k, off):
                            pe.wait_ge(s_trc, t + 1)
                            pe.wait_ge(s_w1, t + 1)
                            if k is not None or t >= 2:
                                pe.wait_ge(s_ra, t - 1)
                                pe.wait_ge(s_rb, t - 1)
                            for c in range(FC):
                                mm = pe.matmul(psum[:, 2 + 2 * par + c % 2, (c // 2) * P:(c // 2 + 1) * P],
                                               w1_now[:, par, c * P:(c + 1) * P], rows_t[:, par, :],
                                               start=True, stop=True)
                            mm.then_inc(s_h, 1)

                        def out(t, par, k, off):
                            e = expert_of(pe, t, k, off)
                            pe.wait_ge(s_ra, t + 1)
                            pe.wait_ge(s_rb, t + 1)
                            if k is not None or t >= 2:
                                pe.wait_ge(s_yc, t - 1)
                            dst_y = psum[:, 6 + par, 0:D]
                            for c in range(FC):
                                pe.matmul(dst_y, hid[:, par, c, :], w2[:, bass.ds(e, 1), c, :],
                                          start=(c == 0), stop=False)
                            mm = pe.matmul(dst_y, ones_f[:], b2[0:1, bass.ds(e, 1), :], start=False, stop=True)
                            mm.then_inc(s_y, 1)

                        turn(0, 0, None, 0)
                        turn(1, 1, None, 0)
                        hidden(0, 0, None, 0)

                        def step(t, par, k, off):
                            turn(t + 2, par, k, off + 2)
                            hidden(t + 1, 1 - par, k, off + 1)
                            out(t, par, k, off)
                        over_tiles(pe, step, 0, tiles - 2)
                        hidden(tiles - 1, (tiles - 1) % 2, None, 0)
                        out(tiles - 2, tiles % 2, None, 0)
                        out(tiles - 1, (tiles - 1) % 2, None, 0)

                    @block.scalar
                    def _(act):
                        def copy_rows(t, par, k, off):
                            act.wait_ge(s_tr, t + 1)
                            if k is not None or t >= 2:
                                act.wait_ge(s_h, t - 1)
                            nc.scalar.copy(rows_t[:, par, :], psum[:, par, 0:P]).then_inc(s_trc, 1)

                        def relu(t, par, k, off):
                            act.wait_ge(s_h, t + 1)
                            if k is not None or t >= 2:
                                act.wait_ge(s_y, t - 1)
                            for c in (0, 2):
                                ins = nc.scalar.activation(hid[:, par, c, :],
                                                           psum[:, 2 + 2 * par, (c // 2) * P:(c // 2 + 1) * P],
                                                           ACT.Relu, bias=w1_now[:, par, F + c:F + c + 1])
                            ins.then_inc(s_ra, 1)

                        def store(t, par, k, off):
                            act.wait_ge(s_y, t + 1)
                            if k is not None or t >= 2:
                                n = t // 2 if k is None else k + off // 2
                                act.wait_ge(s_out[par], 16 * n)
                            nc.scalar.copy(ybuf[:, par, :], psum[:, 6 + par, 0:D]).then_inc(s_yc, 1)
                            act.wait_ge(s_yc, t + 1)
                            act.dma_start(outs_d[layer][bass.ds(t * P, P), :], ybuf[:, par, :]).then_inc(s_out[par], 16)

                        copy_rows(0, 0, None, 0)
                        copy_rows(1, 1, None, 0)
                        relu(0, 0, None, 0)

                        def step(t, par, k, off):
                            copy_rows(t + 2, par, k, off + 2)
                            relu(t + 1, 1 - par, k, off + 1)
                            store(t, par, k, off)
                        over_tiles(act, step, 0, tiles - 2)
                        relu(tiles - 1, (tiles - 1) % 2, None, 0)
                        store(tiles - 2, tiles % 2, None, 0)
                        store(tiles - 1, (tiles - 1) % 2, None, 0)
                        act.wait_ge(s_out[0], 16 * ((tiles + 1) // 2))
                        act.wait_ge(s_out[1], 16 * (tiles // 2))

                    @block.vector
                    def _(dve):
                        def relu(t, par, k, off):
                            dve.wait_ge(s_h, t + 1)
                            if k is not None or t >= 2:
                                dve.wait_ge(s_y, t - 1)
                            for c in (1, 3):
                                ins = dve.tensor_scalar(hid[:, par, c, :],
                                                        psum[:, 3 + 2 * par, (c // 2) * P:(c // 2 + 1) * P],
                                                        w1_now[:, par, F + c:F + c + 1], 0.0, ALU.add, ALU.max)
                            ins.then_inc(s_rb, 1)

                        def choose(t, par, k, off):
                            e = expert_of(dve, t, k, off)
                            if k is not None or t >= 2:
                                dve.wait_ge(s_ra, t - 1)
                                dve.wait_ge(s_rb, t - 1)
                            dve.tensor_scalar(w1_now[:, par:par + 1, :], w1[:, bass.ds(e, 1), :], 1.0, None,
                                              ALU.mult).then_inc(s_w1, 1)

                        dve.wait_ge(s_w[layer], EXPERT_LOADS)
                        choose(0, 0, None, 0)
                        choose(1, 1, None, 0)
                        relu(0, 0, None, 0)

                        def step(t, par, k, off):
                            choose(t + 2, par, k, off + 2)
                            relu(t + 1, 1 - par, k, off + 1)
                        over_tiles(dve, step, 0, tiles - 2)
                        relu(tiles - 1, (tiles - 1) % 2, None, 0)

                with nc.Block() as block:
                    s_g0, s_g, s_ch, s_stats, s_var, s_rstd, s_norm, s_fin = (sm(n) for n in (
                        "cleared", "gathered", "sum_chain", "stats", "var", "rstd", "normed", "stored"))
                    s_gat = [sm(f"gathered{c}") for c in range(NT // KB)]

                    @block.gpsimd
                    def _(pool):
                        if layer == 0:
                            pool.memset(got[:], 0.0).then_inc(s_g0, 1)
                            pool.wait_ge(s_g0, 1)
                        for t in range(NT):
                            pool.indirect_dma_start(
                                got[:, t, :], None, outs_d[layer],
                                bass.IndirectOffsetOnAxis(ap=slot[:, t:t + 1], axis=0),
                                bounds_check=tiles * P - 1, oob_is_err=False).then_inc(s_gat[t // KB], 16)
                        norm_rstd(pool, s_stats, s_var, s_rstd)

                    @block.vector
                    def _(dve):
                        ch = Chain(dve, s_ch)
                        for t in range(NT):
                            if t % KB == 0:
                                dve.wait_ge(s_gat[t // KB], 16 * KB)
                            if layer == 0:
                                ch.step(dve.scalar_tensor_tensor(pre[:, t, :], got[:, t, :], gate[:, t:t + 1],
                                                                 src[:, t, :], ALU.mult, ALU.add))
                            else:
                                ch.step(dve.tensor_tensor(pre[:, t, :], got[:, t, :], src[:, t, :], ALU.add))
                            norm_stats(dve, ch, t).then_inc(s_stats, 1)
                        norm_apply(dve, dst, s_rstd, s_norm)

                    if layer == 1:
                        @block.sync
                        def _(sp):
                            for c in range(NT // KB):
                                sp.wait_ge(s_norm, (c + 1) * KB)
                                sp.dma_start(out_d.rearrange("(t p) d -> p t d", p=P)[:, c * KB:(c + 1) * KB, :],
                                             dst[:, c * KB:(c + 1) * KB, :]).then_inc(s_fin, 16)
                            sp.wait_ge(s_fin, 16 * NT // KB)

        def attend1(src, dst):
            c2 = ExitStack()
            with c2:
                def sb2(name, shape, dt=F32):
                    return c2.enter_context(nc.sbuf_tensor("a1_" + name, shape, dt))

                def sm(name):
                    return sem("a1_" + name)

                lat = sb2("lat", [P, T], F16)
                latv = sb2("latv", [P, NT, 2 * LD + 2], F16)
                y_all = sb2("y_all", [P, NT, H * LD])
                Y1 = 2 * LD + 1

                with ExitStack() as c3, nc.Block() as block:
                    qh = c3.enter_context(nc.sbuf_tensor("a1_qh", [P, 2, T], F16))
                    ql = c3.enter_context(nc.sbuf_tensor("a1_ql", [P, 2, T], F16))
                    s_tr, s_trc, s_p, s_ph, s_pl, s_v, s_vc, s_one = (sm(n) for n in (
                        "turned", "turned_copied", "projected", "high", "low", "latv", "latv_copied", "ones"))
                    s_st = [sm("q_stored_a"), sm("q_stored_b")]
                    CH = T // 512

                    @block.tensor
                    def _(pe):
                        for c in range(NT // KB):
                            for t in range(c * KB, (c + 1) * KB):
                                mm = pe.transpose(psum[:, c, (t % KB) * P:(t % KB + 1) * P], src[:, t, :], ident)
                            mm.then_inc(s_tr, 1)
                        for n in range((G + 1) * CH):
                            g, c = divmod(n, CH)
                            if g == 0:
                                pe.wait_ge(s_trc, c + 1)
                            if n >= 4:
                                pe.wait_ge(s_pl, n - 3)
                            w = wkv_s[:].rearrange("p r c -> p (r c)") if g == 0 else wqk[:, (g - 1) * P:g * P]
                            pe.matmul(psum[:, 4 + n % 4, :], w, xt[:, c * 512:(c + 1) * 512],
                                      start=True, stop=True).then_inc(s_p, 1)
                        for t in range(NT):
                            mm = pe.matmul(psum[:, 0, t * LD:(t + 1) * LD], xt[:, t * P:(t + 1) * P], wkv_s[:, 0, :],
                                           start=True, stop=True)
                        mm.then_inc(s_v, 1)

                    @block.scalar
                    def _(act):
                        for c in range(NT // KB):
                            act.wait_ge(s_tr, c + 1)
                            nc.scalar.copy(xt[:, c * 512:(c + 1) * 512], psum[:, c, :]).then_inc(s_trc, 1)
                        for n in range((G + 1) * CH):
                            g, c = divmod(n, CH)
                            hi = lat if g == 0 else qh[:, (g - 1) % 2, :]
                            act.wait_ge(s_p, n + 1)
                            if g >= 3 and c == 0:
                                act.wait_ge(s_st[(g - 1) % 2], 32)
                            nc.scalar.copy(hi[:, c * 512:(c + 1) * 512], psum[:, 4 + n % 4, :]).then_inc(s_ph, 1)
                        act.wait_ge(s_v, 1)
                        nc.scalar.copy(latv[:, :, 0:LD], psum[:, 0, 0:NT * LD].rearrange("p (t c) -> p t c", c=LD)
                                       ).then_inc(s_vc, 1)

                    @block.vector
                    def _(dve):
                        for n in range((G + 1) * CH):
                            g, c = divmod(n, CH)
                            cols = slice(c * 512, (c + 1) * 512)
                            dve.wait_ge(s_ph, n + 1)
                            if g == 0:
                                for r in (1, 3):
                                    rs = slice(r * LD, (r + 1) * LD)
                                    ins = dve.tensor_tensor(lat[rs, cols], psum[rs, 4 + n % 4, :], lat[rs, cols],
                                                            ALU.subtract)
                                ins.then_inc(s_pl, 1)
                            else:
                                if g >= 3 and c == 0:
                                    dve.wait_ge(s_st[(g - 1) % 2], 32)
                                dve.tensor_tensor(ql[:, (g - 1) % 2, cols], psum[:, 4 + n % 4, :],
                                                  qh[:, (g - 1) % 2, cols], ALU.subtract).then_inc(s_pl, 1)
                        dve.wait_ge(s_vc, 1)
                        dve.tensor_tensor(latv[:, :, LD:2 * LD], psum[:, 0, 0:NT * LD].rearrange("p (t c) -> p t c", c=LD),
                                          latv[:, :, 0:LD], ALU.subtract).then_inc(s_vc, 1)

                    @block.gpsimd
                    def _(pool):
                        pool.memset(latv[:, :, 2 * LD:2 * LD + 2], 1.0).then_inc(s_one, 1)

                    @block.sync
                    def _(sp):
                        for g in range(1, G + 1):
                            sp.wait_ge(s_pl, (g + 1) * CH)
                            for part, q in enumerate((qh, ql)):
                                sp.dma_start(q_d[part][(g - 1) * P:g * P, :], q[:, (g - 1) % 2, :]
                                             ).then_inc(s_st[(g - 1) % 2], 16)
                        for s in s_st:
                            sp.wait_ge(s, 16 * G)
                        load_experts(sp, 1)

                with ExitStack() as c3, nc.Block() as block:
                    def sb3(name, shape, dt=F32):
                        return c3.enter_context(nc.sbuf_tensor("a1_" + name, shape, dt))

                    U = H * B
                    UN = 4
                    NE = 5
                    LAG = 3
                    q = sb3("q", [P, UN, S], F16)
                    nmax = sb3("nmax", [P, UN, 2 * NS])
                    diag = sb3("diag", [P, UN, NS, P], BF16)
                    ex = sb3("ex", [P, NE, S])
                    ex_h = sb3("ex_h", [P, NE, S], F16)
                    ex_l = sb3("ex_l", [P, NE, S], F16)
                    rden = sb3("rden", [P, NS])
                    sums = sb3("sums", [P, 2, NS, Y1])
                    whole = sb3("whole", [P, NS, LD])
                    s_q = [sm(f"q_in{w}") for w in range(UN)]
                    s_ms, s_mt, s_nm, s_dg, s_sc, s_ex, s_ld, s_lp, s_pv, s_sm, s_rd, s_wh, s_y = (sm(n) for n in (
                        "max_scored", "max_taken", "max_ready", "diag", "scored", "exp", "low_dve", "low_pool",
                        "weighed", "sums", "recip", "whole", "y"))
                    pieces = [(i, c, min(512, (i + 1) * P - c)) for i in range(NS) for c in range(0, (i + 1) * P, 512)]
                    NP = len(pieces)
                    groups = [(0,)] + [(j, NS - j) for j in range(1, NS // 2)] + [(NS // 2,)]
                    NG = len(groups)
                    width = [sum(S - j * P for j in g) for g in groups]
                    share = [0] + [(g + 1) * NP // NG for g in range(NG)]

                    def over_units(eng, body):
                        for u in range(UN):
                            body(u, u, u // B)
                        with eng.Fori(1, U // UN - 1) as k:
                            for w in range(UN):
                                body(UN * k + w, w, (UN // B) * k + w // B)
                        for u in range(U - UN, U):
                            body(u, u % UN, u // B)

                    def early(u, n):
                        return isinstance(u, int) and u < n

                    def ending(u, n):
                        return isinstance(u, int) and u + n >= U

                    @block.sync
                    def _(sp):
                        def load(u, w, h):
                            if not early(u, UN):
                                sp.wait_ge(s_sc, NG * (u - UN + 1))
                            b = w % B
                            for r in range(4):
                                sp.dma_start(q[r * LD:(r + 1) * LD, w, :],
                                             q_d[r // 2][bass.ds(h * LD, LD), b * S:(b + 1) * S]).then_inc(s_q[w], 16)
                        over_units(sp, load)

                    @block.tensor
                    def _(pe):
                        def max_piece(u, w, turns, n):
                            i, c, wd = pieces[n]
                            if n == 0:
                                pe.wait_ge(s_q[w], 64 * turns)
                            if not (early(u, 1) and n < 2):
                                pe.wait_ge(s_mt, NP * u + n - 1)
                            b = w % B
                            done = c + wd == (i + 1) * P
                            dst_s = psum[:, n % 2, 0:wd]
                            mm = pe.matmul(dst_s, q[:, w, i * P:(i + 1) * P], lat[:, b * S + c:b * S + c + wd],
                                           start=True, stop=not done)
                            if done:
                                mm = pe.matmul(dst_s[:, wd - P:wd], ident_b, mask_qk, start=False, stop=True)
                            mm.then_inc(s_ms, 1)

                        def score(u, w, g, bank):
                            b = w % B
                            if g == 0 and bank == 0:
                                pe.wait_ge(s_dg, NS * (u + 1))
                            if bank == 0 and not (early(u, 1) and g < 2):
                                pe.wait_ge(s_ex, NG * u + g - 1)
                            at = 0
                            for j in groups[g]:
                                lo = j * P
                                while lo < S:
                                    k = min(S - lo, 512 - at % 512)
                                    if at // 512 != bank:
                                        lo, at = lo + k, at + k
                                        continue
                                    dst_s = psum[:, 2 + 2 * ((NG * w + g) % 2) + at // 512, at % 512:at % 512 + k]
                                    pe.matmul(dst_s, lat[:, b * S + j * P:b * S + (j + 1) * P], q[:, w, lo:lo + k],
                                              start=True, stop=False)
                                    diagonal = lo == j * P
                                    mm = pe.matmul(dst_s, ones_b,
                                                   diag[:, w, lo // P:(lo + k) // P, :].rearrange("p a n -> p (a n)"),
                                                   start=False, stop=not diagonal)
                                    if diagonal:
                                        mm = pe.matmul(dst_s[:, 0:P], ident_b, mask_kq, start=False, stop=True)
                                    lo, at = lo + k, at + k
                            if bank == (width[g] - 1) // 512:
                                mm.then_inc(s_sc, 1)

                        def weigh(u, w, g, part_of_two):
                            b = w % B
                            if part_of_two == 1:
                                pass
                            elif g == NG - 1:
                                pe.wait_ge(s_ld, u + 1)
                            else:
                                pe.wait_ge(s_lp, (NG - 1) * u + g + 1)
                                if g == 0 and not early(u, 1):
                                    pe.wait_ge(s_sm, u)
                            blocks = [(j, i) for j in groups[g] for i in range(j, NS)]
                            half = len(blocks) // 2
                            for n in range(part_of_two * half, part_of_two * half + half):
                                j, i = blocks[n]
                                for part, e in enumerate((ex_h, ex_l)):
                                    mm = pe.matmul(psum[:, 6 + i // 4, (i % 4) * Y1:(i % 4 + 1) * Y1],
                                                   e[:, (NG * w + g) % NE, n * P:(n + 1) * P], latv[:, b * NS + j, 0:Y1],
                                                   start=(j == 0 and i % 4 == 0 and part == 0),
                                                   stop=(j == i and part == 1), skip_group_check=True)
                            if part_of_two == 1:
                                mm.then_inc(s_pv, 1)

                        for u in range(2):
                            for n in range(NP):
                                max_piece(u, u, 1, n)

                        def unit(u, w, k):
                            for g in range(NG):
                                todo = [] if ending(u, 2) else list(range(share[g], share[g + 1]))

                                def some_max(last=False):
                                    while todo:
                                        max_piece(u + 2, (w + 2) % UN, k + 1 + (w + 2) // UN, todo.pop(0))
                                        if not last:
                                            break

                                def some_weigh(part_of_two):
                                    if g >= LAG:
                                        weigh(u, w, g - LAG, part_of_two)
                                    elif not early(u, 1):
                                        weigh(u - 1, (w - 1) % UN, g - LAG + NG, part_of_two)

                                score(u, w, g, 0)
                                some_max()
                                if width[g] > 512:
                                    score(u, w, g, 1)
                                    some_max()
                                some_weigh(0)
                                some_max(last=True)
                                some_weigh(1)

                        for u in range(UN):
                            unit(u, u, 0)
                        with pe.Fori(1, U // UN - 1) as k:
                            for w in range(UN):
                                unit(UN * k + w, w, k)
                        for u in range(U - UN, U):
                            unit(u, u % UN, u // UN)
                        for g in range(NG - LAG, NG):
                            weigh(U - 1, UN - 1, g, 0)
                            weigh(U - 1, UN - 1, g, 1)

                    @block.scalar
                    def _(act):
                        def copy_sums(u, b):
                            if not early(u, 2):
                                act.wait_ge(s_y, u - 1)
                            act.wait_ge(s_pv, NG * (u + 1))
                            nc.scalar.copy(sums[:, b].rearrange("p (a i) c -> p a (i c)", a=2),
                                           psum[:, 6:8, 0:4 * Y1]).then_inc(s_sm, 1)

                        def unit(u, w, h):
                            for g in range(NG):
                                if g == LAG and not early(u, 1):
                                    copy_sums(u - 1, (w - 1) % B)
                                n = NG * w + g
                                wd = width[g]
                                scores = psum[:, 2 + 2 * (n % 2):4 + 2 * (n % 2), :].rearrange("p a n -> p (a n)")[:, 0:wd]
                                if not (early(u, 1) and g < NE):
                                    act.wait_ge(s_pv, NG * u + g - NE + 1)
                                act.wait_ge(s_sc, NG * u + g + 1)
                                nc.scalar.activation(ex[:, n % NE, 0:wd], scores, ACT.Exp, scale=SCALE1)
                                nc.scalar.activation(ex_h[:, n % NE, 0:wd], scores, ACT.Exp,
                                                     scale=SCALE1).then_inc(s_ex, 1)
                        over_units(act, unit)
                        copy_sums(U - 1, B - 1)

                    def low_part(eng, w, g):
                        n = (NG * w + g) % NE
                        return eng.tensor_tensor(ex_l[:, n, 0:width[g]], ex[:, n, 0:width[g]], ex_h[:, n, 0:width[g]],
                                                 ALU.subtract)

                    @block.vector
                    def _(dve):
                        def maximum(u, w, n):
                            i, c, wd = pieces[n]
                            if n == 0 and not early(u, UN):
                                dve.wait_ge(s_dg, NS * (u - UN + 1))
                            dve.wait_ge(s_ms, NP * u + n + 1)
                            dve.tensor_reduce(nmax[:, w, i + NS * (c // 512):i + NS * (c // 512) + 1],
                                              psum[:, n % 2, 0:wd], AX.X, ALU.max, negate=True).then_inc(s_mt, 1)
                            if n == NP - 1:
                                dve.wait_ge(s_mt, NP * (u + 1))
                                two = NS // 2
                                dve.tensor_tensor(nmax[:, w, two:NS], nmax[:, w, two:NS],
                                                  nmax[:, w, NS + two:2 * NS], ALU.min).then_inc(s_nm, 1)

                        def diagonal(u, w, i):
                            if i == 0:
                                dve.wait_ge(s_nm, u + 1)
                                if not early(u, UN):
                                    dve.wait_ge(s_sc, NG * (u - UN + 1))
                            dve.tensor_scalar(diag[:, w, i, :], ident_b, nmax[:, w, i:i + 1], None,
                                              ALU.mult).then_inc(s_dg, 1)

                        def last_low(u, w):
                            dve.wait_ge(s_ex, NG * (u + 1))
                            low_part(dve, w, NG - 1).then_inc(s_ld, 1)

                        def output_whole(u, b):
                            dve.wait_ge(s_sm, u + 1)
                            dve.tensor_tensor(whole[:], sums[:, b, :, 0:LD], sums[:, b, :, LD:2 * LD], ALU.add
                                              ).then_inc(s_wh, 1)

                        def output_recip(u, b):
                            dve.reciprocal(rden[:], sums[:, b, :, 2 * LD]).then_inc(s_rd, 1)

                        def output_scaled(u, b, h):
                            dve.wait_ge(s_wh, u + 1)
                            dve.wait_ge(s_rd, u + 1)
                            dve.tensor_tensor(y_all[:, b * NS:(b + 1) * NS, bass.ds(h * LD, LD)], whole[:],
                                              rden[:].unsqueeze(2).broadcast_to((P, NS, LD)), ALU.mult).then_inc(s_y, 1)

                        for u in range(2):
                            for n in range(NP):
                                maximum(u, u, n)
                        for i in range(NS):
                            diagonal(0, 0, i)

                        def unit(u, w, h):
                            for n in range(NP):
                                if not ending(u, 2):
                                    maximum(u + 2, (w + 2) % UN, n)
                                if n < NS and not ending(u, 1):
                                    diagonal(u + 1, (w + 1) % UN, n)
                                if not early(u, 1):
                                    if n == 1:
                                        last_low(u - 1, (w - 1) % UN)
                                    if n == NP - 3:
                                        output_whole(u - 1, (w - 1) % B)
                                    if n == NP - 2:
                                        output_recip(u - 1, (w - 1) % B)
                                    if n == NP - 1:
                                        output_scaled(u - 1, (w - 1) % B, h if w % B else h - 1)
                        over_units(dve, unit)
                        last_low(U - 1, UN - 1)
                        output_whole(U - 1, B - 1)
                        output_recip(U - 1, B - 1)
                        output_scaled(U - 1, B - 1, H - 1)

                    @block.gpsimd
                    def _(pool):
                        def unit(u, w, h):
                            for g in range(NG - 1):
                                pool.wait_ge(s_ex, NG * u + g + 1)
                                low_part(pool, w, g).then_inc(s_lp, 1)
                        over_units(pool, unit)

                with ExitStack() as c3, nc.Block() as block:
                    yt = c3.enter_context(nc.sbuf_tensor("a1_yt", [P, 2, G, P], F32))
                    s_tr, s_trc, s_o, s_oc, s_ch, s_stats, s_var, s_rstd, s_norm = (sm("o_" + n) for n in (
                        "turned", "copied", "out", "taken", "chain", "stats", "var", "rstd", "normed"))

                    @block.tensor
                    def _(pe):
                        def turn(t):
                            if t >= 2:
                                pe.wait_ge(s_trc, t - 1)
                            for g in range(G):
                                mm = pe.transpose(psum[:, t % 2, g * P:(g + 1) * P], y_all[:, t, g * P:(g + 1) * P], ident)
                            mm.then_inc(s_tr, 1)
                        turn(0)
                        for t in range(NT):
                            if t + 1 < NT:
                                turn(t + 1)
                            pe.wait_ge(s_trc, t + 1)
                            if t >= 2:
                                pe.wait_ge(s_oc, t - 1)
                            for g in range(G):
                                mm = pe.matmul(psum[:, 2 + t % 2, 0:D], yt[:, t % 2, g, :], wvo[:, g, :],
                                               start=(g == 0), stop=(g == G - 1))
                            mm.then_inc(s_o, 1)

                    @block.scalar
                    def _(act):
                        for t in range(NT):
                            act.wait_ge(s_tr, t + 1)
                            if t >= 2:
                                act.wait_ge(s_o, t - 1)
                            nc.scalar.copy(yt[:, t % 2], psum[:, t % 2, :].rearrange("p (g q) -> p g q", q=P)
                                           ).then_inc(s_trc, 1)

                    @block.vector
                    def _(dve):
                        ch = Chain(dve, s_ch)
                        for t in range(NT):
                            dve.wait_ge(s_o, t + 1)
                            dve.tensor_tensor(pre[:, t, :], psum[:, 2 + t % 2, 0:D], src[:, t, :], ALU.add
                                              ).then_inc(s_oc, 1)
                            dve.wait_ge(s_oc, t + 1)
                            norm_stats(dve, ch, t).then_inc(s_stats, 1)
                        norm_apply(dve, dst, s_rstd, s_norm)

                    @block.gpsimd
                    def _(pool):
                        norm_rstd(pool, s_stats, s_var, s_rstd)

        attend0()
        experts(0, xa, xb)
        attend1(xb, xa)
        experts(1, xa, xb)


def constants(T, E, tiles):
    import numpy as np
    NT = T // P
    f = np.zeros((P, 4 * P + NT * E + E * NT + 32), np.float32)
    f[:, 0:P] = np.eye(P)
    f[:, P:P + NT * E] = np.tile(E - np.arange(E), NT)
    f[:, 2 * P:2 * P + E * NT] = np.tile(P * np.arange(NT), E)
    f[:, 3 * P:3 * P + tiles * E] = np.repeat(np.arange(tiles), E)
    f[:, 3 * P + tiles * E:3 * P + tiles * E + NT] = -0.5
    i = np.arange(P)
    b = np.concatenate([np.eye(P), np.ones((P, P)), (i[:, None] <= i[None, :]),
                        np.where(i[None, :] > i[:, None], NEG, 0.0),
                        np.where(i[:, None] > i[None, :], NEG, 0.0)], axis=1).astype(np.float32)
    return f, b


def kernel(**inputs):
    import numpy as np
    import concourse.bacc as bacc
    from concourse.bass_utils import run_bass_kernel_spmd

    a = {k: np.asarray(v) for k, v in inputs.items()}
    x = a["L0_attn_x"]
    B, S, Dm = x.shape
    E = a["L0_ffn_router_w"].shape[1]
    rows = x.reshape(B * S, Dm)

    def bias_columns(b1):
        e, f = b1.shape
        return b1.reshape(e, f // P, P).transpose(2, 0, 1).reshape(P, -1)

    const_f, const_b = constants(B * S, E, B * S // P + E - 1)
    arrays = {
        "x_tok": rows, "x_t": rows.T,
        "wq0": a["L0_attn_Wq"], "wk0": a["L0_attn_Wk"], "wv0_t": a["L0_attn_Wv"].T,
        "router": a["L0_ffn_router_w"],
        "w1a": a["L0_ffn_w1"], "b1a": bias_columns(a["L0_ffn_b1"]), "w2a": a["L0_ffn_w2"], "b2a": a["L0_ffn_b2"],
        "wq1_t": a["L1_attn_Wq"].transpose(2, 1, 0), "wkv": a["L1_attn_Wkv_down"],
        "wku_t": a["L1_attn_Wk_up"].transpose(2, 1, 0), "wvu_t": a["L1_attn_Wv_up"].transpose(2, 1, 0),
        "wout": a["L1_attn_Wout"].transpose(1, 0, 2),
        "gate_w_t": a["L1_ffn_gate_w"].T, "gate_b": a["L1_ffn_gate_b"],
        "w1b": a["L1_ffn_w1"].transpose(0, 2, 1), "b1b": bias_columns(a["L1_ffn_b1"]),
        "w2b": a["L1_ffn_w2"].transpose(0, 2, 1), "b2b": a["L1_ffn_b2"],
        "const_f": const_f, "const_b": const_b,
    }
    nc = bacc.Bacc("TRN2", target_bir_lowering=False, num_devices=1)
    arrays = {f"in_{k}": np.ascontiguousarray(v) for k, v in arrays.items()}
    args = [nc.dram_tensor(k, v.shape, mybir.dt.from_np(v.dtype), kind="ExternalInput").ap() for k, v in arrays.items()]
    out = nc.dram_tensor("out_dram", (B * S, Dm), F32, kind="ExternalOutput").ap()
    build(nc, *args, out)
    r = run_bass_kernel_spmd(nc, [arrays], core_ids=[0])
    return r.results[0]["out_dram"].reshape(B, S, Dm)
```

```python
from contextlib import ExitStack

import concourse.bass as bass
from concourse import mybir

ALU = mybir.AluOpType
ACT = mybir.ActivationFunctionType
AX = mybir.AxisListType
F32 = mybir.dt.float32
F16 = mybir.dt.float16
BF16 = mybir.dt.bfloat16
I32 = mybir.dt.int32

P = 128
D = 128
EPS = 1e-5
NEG = -1e38
KB = 4


def build(nc, x_tok_d, x_t_d, wq0, wk0, wv0_t, router, w1a_d, b1a_d, w2a_d, b2a_d,
          wq1_t, wkv, wku_t, wvu_t, wout, gate_w_t, gate_b, w1b_d, b1b_d, w2b_d, b2b_d,
          const_f_d, const_b_d, out_d):
    T = x_tok_d.shape[0]
    B = 2
    S = T // B
    NT = T // P
    NS = S // P
    E = router.shape[1]
    F = w1a_d.shape[2]
    FC = F // P
    W1 = F + FC
    H, HD, LD = wq1_t.shape[1], wq1_t.shape[0], wkv.shape[1]
    G = H * LD // P
    HG = H // G
    CAP = max(round(T / E), 4)
    TILES = (E * CAP // P, NT + E - 1)
    SCALE0, SCALE1 = float(D) ** -0.5, float(HD) ** -0.5

    ctx = ExitStack()
    with ctx:
        def sb(name, shape, dt=F32):
            return ctx.enter_context(nc.sbuf_tensor(name, shape, dt))

        def sem(name):
            return ctx.enter_context(nc.semaphore(name))

        x0 = sb("x0", [P, NT, D])
        xt = sb("xt", [P, T])
        row_bufs = sb("row_bufs", [P, 4, D + 1])
        pre = sb("pre", [P, NT, D])
        xa_gate = sb("xa_gate", [P, NT, D + 1])
        xa = xa_gate[:, :, 0:D]
        xb = sb("xb", [P, NT, D])
        stats = sb("stats", [P, NT, 6])
        mv = sb("mv", [P, NT, 2])
        var = sb("var", [P, NT])
        rstd = sb("rstd", [P, NT])

        cf = sb("cf", [P, 4 * P + NT * E + E * NT + E * E])
        ident = cf[:, 0:P]
        rank = cf[:, P:P + NT * E].rearrange("p (t e) -> p t e", e=E)
        edge = cf[:, 2 * P:2 * P + E * NT].rearrange("p (e j) -> p e j", j=NT)
        tile_no = cf[:, 3 * P:3 * P + TILES[1] * E].rearrange("p (t e) -> p t e", e=E)
        more_cols = 3 * P + TILES[1] * E
        half = cf[:, more_cols:more_cols + NT]
        code_t = cf[:, more_cols + NT:more_cols + 2 * NT]
        code_p = cf[:, more_cols + 2 * NT:more_cols + 2 * NT + 1]
        earlier_at = more_cols + 2 * NT + 1
        earlier = cf[:, earlier_at:earlier_at + E * E].rearrange("p (e f) -> p e f", f=E)
        cb = sb("cb", [P, 6 * P], BF16)
        ident_b, ones_b, upper_b = (cb[:, i * P:(i + 1) * P] for i in range(3))
        mask_qk, mask_kq = (cb[:, i * P:(i + 1) * P] for i in range(3, 5))
        low_row = cb[:, 5 * P:6 * P]
        ones_f = sb("ones_f", [1, P])

        w1 = sb("w1", [P, E, W1])
        w2 = sb("w2", [P, E, FC, D])
        b2 = sb("b2", [1, E, D])
        rt = sb("rt", [P, 2, E])
        gb = sb("gb", [1, E])
        wsm = sb("wsm", [P, 3, P])
        wkv_s = sb("wkv_s", [P, 4, LD])
        wqk = sb("wqk", [P, H * LD])
        y_all = sb("y_all", [P, NT, H * LD])
        HW = P + 2 * LD + D
        hw = y_all[0:HD].rearrange("p t c -> p (t c)")[:, 0:H * HW].rearrange("p (h n) -> p h n", n=HW)
        wvo = sb("wvo", [P, G, D])

        psum = ctx.enter_context(nc.psum_tensor("psum", [P, 8, 512], F32))

        rows_d = [nc.dram_tensor("rows0", [T, D + 1], F32, kind="Internal").ap(),
                  nc.dram_tensor("rows1", [T, D], F32, kind="Internal").ap()]
        x2_d = nc.dram_tensor("x2", [T, D], F32, kind="Internal").ap()
        q_d = nc.dram_tensor("q_parts", [2, H * LD, T], F16, kind="Internal").ap()

        s_first = sem("first_weights_in")
        s_small = sem("small_weights_in")
        s_x = sem("x_in")
        s_xt = [sem("x_turned_in_a"), sem("x_turned_in_b")]
        s_w = [sem("experts0_in"), sem("experts1_in")]
        s_heads = sem("head_weights_in")
        s_rows = [sem("rows0_stored"), sem("rows1_stored")]
        s_alone = sem("alone_stored")

        def load_experts(eng, layer):
            w1_d, b1_d, w2_d, b2_d = ((w1a_d, b1a_d, w2a_d, b2a_d), (w1b_d, b1b_d, w2b_d, b2b_d))[layer]
            eng.dma_start(w1[:, :, 0:F], w1_d.rearrange("e d f -> d e f")).then_inc(s_w[layer], 16)
            eng.dma_start(w1[:, :, F:W1], b1_d.rearrange("p (e c) -> p e c", c=FC)).then_inc(s_w[layer], 16)
            for e in range(E):
                eng.dma_start(w2[:, e], w2_d[e].rearrange("(c p) d -> p c d", p=P)).then_inc(s_w[layer], 16)
            eng.dma_start(b2[:], b2_d.rearrange("(o e) d -> o e d", o=1)).then_inc(s_w[layer], 16)

        EXPERT_LOADS = 16 * (3 + E)

        class Norm:

            def __init__(self, name, dst, src=None, src_ready=None):
                self.dst, self.src = dst, pre if src is None else src
                self.bn, self.stats, self.var, self.rstd, self.done = (sem(f"{name}_{n}") for n in (
                    "bn", "stats", "var", "rstd", "normed"))
                self.pre = src_ready or sem(f"{name}_pre")

            def take(self, dve, t):
                dve.wait_ge(self.pre, t + 1)
                dve.bn_stats(stats[:, t, :], self.src[:, t, :]).then_inc(self.bn, 1)
                dve.wait_ge(self.bn, t + 1)
                dve.bn_aggr(mv[:, t, :], stats[:, t, :]).then_inc(self.stats, 1)

            def root(self, pool, c):
                ts = slice(c * KB, (c + 1) * KB)
                pool.wait_ge(self.stats, KB * (c + 1))
                pool.tensor_scalar(var[:, ts], mv[:, ts, 1], EPS, None, ALU.add).then_inc(self.var, 1)
                pool.wait_ge(self.var, c + 1)
                pool.tensor_tensor(rstd[:, ts], var[:, ts], half[:, ts], ALU.pow).then_inc(self.rstd, 1)

            def apply(self, dve, c):
                dve.wait_ge(self.rstd, c + 1)
                for t in range(c * KB, (c + 1) * KB):
                    dve.tensor_scalar(self.dst[:, t, :], self.src[:, t, :], mv[:, t, 0:1], rstd[:, t:t + 1],
                                      ALU.subtract, ALU.mult).then_inc(self.done, 1)

        lg = sb("lg", [P, NT, E])
        top = sb("top", [P, NT])
        hit = sb("hit", [P, NT, E])
        cand = sb("cand", [P, NT, E])
        best = sb("best", [P, NT])
        pick = sb("pick", [P, NT, E])
        pick_b = sb("pick_b", [P, NT, E], BF16)
        soft = sb("soft", [P, NT, E])
        den_r = sb("den_r", [P, NT])
        cnt = sb("cnt", [P, NT, E])
        count = sb("count", [P, NT])
        full = sb("full", [P, NT, NT])
        nth = sb("nth", [P, NT])
        low = sb("low", [P, NT])
        over = sb("over", [P, NT])
        high = sb("high", [P, NT])
        in_tile = sb("in_tile", [P, NT, max(TILES)], BF16)
        hot_low = sb("hot_low", [P, NT, P], BF16)
        hot_high = sb("hot_high", [P, NT, 2 * max(TILES)], BF16)
        table_f = sb("table_f", [P, max(TILES)])
        table = sb("table", [P, max(TILES)], I32)
        owner = sb("owner", [1, max(TILES)], I32)
        tot = sb("tot", [P, E])
        more = sb("more", [P, E, NT])
        used = sb("used", [P, E])
        before = sb("before", [P, E, E])
        ends = sb("ends", [P, E])
        offs = sb("offs", [P, E])
        past = sb("past", [1, max(TILES), E])
        own_f = sb("own_f", [1, max(TILES)])
        xr = sb("xr", [P, 512])

        class Route:

            def __init__(self, layer, norm, bank):
                self.layer, self.norm, self.bank = layer, norm, bank
                self.tiles = TILES[layer]
                (self.tr, self.trc, self.lg, self.ch, self.pick, self.cnt, self.cntd, self.dif, self.ex, self.gate,
                 self.hot, self.sum, self.table) = (sem(f"r{layer}_{n}") for n in (
                     "turned", "turned_copied", "logits", "chain", "picked", "counted", "count_taken", "dif", "exp",
                     "gate", "hot_rows", "table_summed", "table"))
                self.n = 0

            def turn(self, pe, c):
                pe.wait_ge(self.norm.done, KB * (c + 1))
                if c >= 1:
                    pe.wait_ge(self.cntd, c)
                for t in range(KB):
                    mm = pe.transpose(psum[:, self.bank, t * P:(t + 1) * P], self.norm.dst[:, c * KB + t, :], ident)
                mm.then_inc(self.tr, 1)

            def copy(self, act, c):
                act.wait_ge(self.tr, c + 1)
                if c >= 1:
                    act.wait_ge(self.lg, c)
                nc.scalar.copy(xr[:], psum[:, self.bank, :]).then_inc(self.trc, 1)

            def logits(self, pe, c):
                pe.wait_ge(self.trc, c + 1)
                for t in range(KB):
                    dst = psum[:, self.bank, t * E:(t + 1) * E]
                    mm = pe.matmul(dst, xr[:, t * P:(t + 1) * P], rt[:, self.layer, :], start=True,
                                   stop=(self.layer == 0))
                    if self.layer == 1:
                        mm = pe.matmul(dst, ones_f[:], gb[:], start=False, stop=True)
                mm.then_inc(self.lg, 1)

            def step(self, dve, ins):
                self.n += 1
                ins.then_inc(self.ch, 1)
                dve.wait_ge(self.ch, self.n)

            def choose(self, dve, c):
                ts = slice(c * KB, (c + 1) * KB)

                def wide(a):
                    return a.unsqueeze(2).broadcast_to((P, KB, E))

                dve.wait_ge(self.lg, c + 1)
                self.step(dve, dve.tensor_copy(lg[:, ts], psum[:, self.bank, 0:KB * E].rearrange("p (t e) -> p t e", e=E)))
                self.step(dve, dve.tensor_reduce(top[:, ts], lg[:, ts], AX.X, ALU.max))
                self.step(dve, dve.tensor_tensor(hit[:, ts], lg[:, ts], wide(top[:, ts]), ALU.is_equal))
                self.step(dve, dve.tensor_tensor(cand[:, ts], hit[:, ts], rank[:, ts], ALU.mult))
                self.step(dve, dve.tensor_reduce(best[:, ts], cand[:, ts], AX.X, ALU.max))
                self.step(dve, dve.tensor_tensor(pick[:, ts], rank[:, ts], wide(best[:, ts]), ALU.is_equal))
                dve.tensor_copy(pick_b[:, ts], pick[:, ts]).then_inc(self.pick, 1)
                if self.layer == 0:
                    dve.tensor_tensor(soft[:, ts], lg[:, ts], wide(top[:, ts]), ALU.subtract).then_inc(self.dif, 1)

            def exp(self, act, c):
                ts = slice(c * KB, (c + 1) * KB)
                act.wait_ge(self.dif, c + 1)
                nc.scalar.activation(soft[:, ts], soft[:, ts], ACT.Exp).then_inc(self.ex, 1)

            def tally(self, pe, c):
                pe.wait_ge(self.pick, c + 1)
                at = 2 * P
                picks = [pick_b[:, t, :] for t in range(NT)]
                pe.matmul(psum[:, self.bank, at:at + KB * E], upper_b,
                          pick_b[:, c * KB:(c + 1) * KB, :].rearrange("p t e -> p (t e)"), start=True, stop=False)
                for s in range(1, KB):
                    mm = pe.matmul(psum[:, self.bank, at + s * E:at + KB * E], ones_b,
                                   pick_b[:, c * KB:(c + 1) * KB - s, :].rearrange("p t e -> p (t e)"),
                                   start=False, stop=(c == 0 and s == KB - 1))
                for t in range(c * KB):
                    mm = pe.matmul(psum[:, self.bank, at:at + KB * E], ones_b,
                                   picks[t].unsqueeze(1).broadcast_to((P, KB, E)), start=False, stop=(t == c * KB - 1))
                if self.layer == 1 and c == NT // KB - 1:
                    for t in range(NT):
                        mm = pe.matmul(psum[:, self.bank, at + P:at + P + E], ones_b, picks[t],
                                       start=(t == 0), stop=(t == NT - 1))
                mm.then_inc(self.cnt, 1)

            def settle(self, dve, c):
                ts = slice(c * KB, (c + 1) * KB)
                at = 2 * P
                dve.wait_ge(self.cnt, c + 1)
                if self.layer == 1 and c == NT // KB - 1:
                    self.step(dve, dve.tensor_copy(tot[:], psum[:, self.bank, at + P:at + P + E]))
                dve.tensor_tensor(cnt[:, ts], psum[:, self.bank, at:at + KB * E].rearrange("p (t e) -> p t e", e=E),
                                  pick[:, ts], ALU.mult).then_inc(self.cntd, 1)
                if self.layer == 0:
                    dve.wait_ge(self.ex, c + 1)
                    self.step(dve, dve.tensor_reduce(den_r[:, ts], soft[:, ts], AX.X, ALU.add))
                    dve.reciprocal(xa_gate[:, ts, D], den_r[:, ts]).then_inc(self.gate, 1)
                dve.wait_ge(self.cntd, c + 1)
                self.step(dve, dve.tensor_reduce(count[:, ts], cnt[:, ts], AX.X, ALU.add))
                self.step(dve, dve.tensor_tensor(full[:, ts], count[:, ts].unsqueeze(2).broadcast_to((P, KB, NT)),
                                                 edge[:, 0:KB], ALU.is_gt))
                self.step(dve, dve.tensor_reduce(nth[:, ts], full[:, ts], AX.X, ALU.add))
                self.step(dve, dve.scalar_tensor_tensor(low[:, ts], nth[:, ts], -float(P), count[:, ts],
                                                        ALU.mult, ALU.add))
                for t in range(c * KB, (c + 1) * KB):
                    ins = dve.tensor_scalar(hot_low[:, t, :], low_row, low[:, t:t + 1], None, ALU.is_equal)
                if self.layer == 1:
                    ins.then_inc(self.hot, KB)
                    return
                held = CAP // P
                dve.scalar_tensor_tensor(high[:, ts], best[:, ts], -float(held), nth[:, ts], ALU.mult, ALU.add
                                         ).then_inc(self.ch, 1)
                self.step(dve, dve.tensor_scalar(over[:, ts], nth[:, ts], float(held), float(E * held),
                                                 ALU.is_gt, ALU.mult))
                self.n += 1
                dve.wait_ge(self.ch, self.n)
                self.step(dve, dve.scalar_tensor_tensor(high[:, ts], over[:, ts], float(E * held - 1), high[:, ts],
                                                        ALU.add, ALU.add))
                self.high_rows(dve, ts, KB)

            def high_rows(self, dve, ts, n):
                k = self.tiles
                self.step(dve, dve.tensor_tensor(in_tile[:, ts, 0:k],
                                                 tile_no[:, 0:k, 0].unsqueeze(1).broadcast_to((P, n, k)),
                                                 high[:, ts].unsqueeze(2).broadcast_to((P, n, k)), ALU.is_equal))
                dve.tensor_scalar(hot_high[:, ts, 0:k], in_tile[:, ts, 0:k], code_p, None, ALU.mult)
                dve.tensor_tensor(hot_high[:, ts, k:2 * k], in_tile[:, ts, 0:k],
                                  code_t[:, ts].unsqueeze(2).broadcast_to((P, n, k)), ALU.mult).then_inc(self.hot, n)

            def sum_table(self, pe):
                k = self.tiles
                pe.wait_ge(self.hot, NT * (1 + self.layer))
                for t in range(NT):
                    mm = pe.matmul(psum[:, self.bank, 0:2 * k], hot_low[:, t, :], hot_high[:, t, 0:2 * k],
                                   start=(t == 0), stop=(t == NT - 1))
                mm.then_inc(self.sum, 1)

            def take_table(self, dve):
                k = self.tiles
                dve.wait_ge(self.sum, 1)
                self.step(dve, dve.tensor_scalar(table_f[:, 0:k], psum[:, self.bank, k:2 * k], float(P), float(T),
                                                 ALU.mult, ALU.add))
                dve.tensor_tensor(table[:, 0:k], table_f[:, 0:k], psum[:, self.bank, 0:k], ALU.add
                                  ).then_inc(self.table, 1)

            def settle_all(self, dve):
                tiles = TILES[1]
                self.step(dve, dve.tensor_tensor(more[:], tot[:].unsqueeze(2).broadcast_to((P, E, NT)), edge, ALU.is_gt))
                self.step(dve, dve.tensor_reduce(used[:], more[:], AX.X, ALU.add))
                self.step(dve, dve.tensor_tensor(before[:], used[:].unsqueeze(1).broadcast_to((P, E, E)), earlier, ALU.mult))
                self.step(dve, dve.tensor_reduce(offs[:], before[:], AX.X, ALU.add))
                self.step(dve, dve.tensor_tensor(cnt[:], pick[:], offs[:].unsqueeze(1).broadcast_to((P, NT, E)), ALU.mult))
                self.step(dve, dve.tensor_reduce(high[:], cnt[:], AX.X, ALU.add))
                self.step(dve, dve.scalar_tensor_tensor(high[:], high[:], -1.0, nth[:], ALU.add, ALU.add))
                self.high_rows(dve, slice(0, NT), NT)
                self.step(dve, dve.tensor_tensor(ends[:], offs[:], used[:], ALU.add))
                self.step(dve, dve.tensor_tensor(past[:], ends[0:1, :].unsqueeze(1).broadcast_to((1, tiles, E)),
                                                 tile_no[0:1, 0:tiles, :], ALU.is_le))
                self.step(dve, dve.tensor_reduce(own_f[:], past[:], AX.X, ALU.add))
                self.step(dve, dve.tensor_scalar(own_f[:], own_f[:], float(E - 1), None, ALU.min))
                self.step(dve, dve.tensor_copy(owner[:], own_f[:]))
                self.take_table(dve)

        GROUPS = NT // KB

        def groups_due(i, lag, more=0):
            return [c for c in range(GROUPS) if i == KB * (c + 1) - 1 + lag + (more if c < GROUPS - 2 else 0)]

        def by_group(rows, c):
            return rows.rearrange("(t p) d -> p t d", p=P)[:, c * KB:(c + 1) * KB, :]

        norm0 = Norm("n0", xa)
        route0 = Route(0, norm0, 7)
        ALONE = GROUPS - 2
        alone = Norm("alone", xb, src=xa, src_ready=norm0.done)
        norm2 = Norm("n2", xa)
        route1 = Route(1, norm2, 4)
        routes = (route0, route1)

        def store_alone(eng, c):
            eng.wait_ge(alone.done, KB * (c + 1))
            eng.dma_start(by_group(x2_d, c), xb[:, c * KB:(c + 1) * KB, :]).then_inc(s_alone, 16)

        def attend0():
            c2 = ExitStack()
            with c2, nc.Block() as block:
                def sb2(name, shape, dt=F32):
                    return c2.enter_context(nc.sbuf_tensor(name, shape, dt))

                qk = sb2("qk", [P, P])
                qt = sb2("qt", [P, T])
                v = sb2("v", [P, NT, D])
                prob = sb2("prob", [P, 2, S])
                prob_t = sb2("prob_t", [P, 2, NS, P])
                m = sb2("m", [P, NT])
                nm = sb2("nm", [P, NT])
                den = sb2("den", [P, NT])
                rden = sb2("rden", [P, NT])
                cb_f = sb2("cb_f", [P, 6 * P])
                s_qk, s_qkc, s_qt, s_qtc, s_v, s_vc = (sem("a0_" + n) for n in
                                                       ("qk", "qk_copied", "q", "q_copied", "v", "v_copied"))
                s_sc, s_m, s_nm, s_exp, s_tr, s_trc, s_o = (sem("a0_" + n) for n in (
                    "scored", "max", "neg_max", "exp", "turned", "turned_copied", "out"))
                s_rd = sem("a0_recip")
                norm, route = norm0, route0
                TURNS = NT + 9
                s_ones, s_cb_in, s_cb, s_hq, s_hqc = (sem("a0_" + n) for n in (
                    "ones", "masks_in", "masks", "head_queries", "head_queries_copied"))
                first = [sum((r % NS) // KB + 1 for r in range(i)) for i in range(NT + 1)]

                @block.sync
                def _(sp):
                    sp.dma_start(wsm[:, 0, :], wq0).then_inc(s_first, 16)
                    sp.dma_start(wsm[:, 1, :], wk0).then_inc(s_first, 16)
                    for c in range(2):
                        sp.dma_start(xt[:, c * S:(c + 1) * S], x_t_d[:, c * S:(c + 1) * S]).then_inc(s_xt[c], 16)
                    sp.dma_start(x0[:], x_tok_d.rearrange("(t p) d -> p t d", p=P)).then_inc(s_x, 16)
                    for r in range(4):
                        sp.dma_start(wkv_s[:, r, :], wkv).then_inc(s_small, 16)
                    sp.dma_start(hw[:, :, 0:P], wq1_t).then_inc(s_heads, 16)
                    sp.dma_start(hw[:, :, P:P + LD], wku_t).then_inc(s_heads, 16)
                    sp.dma_start(hw[:, :, P + LD:P + 2 * LD], wvu_t).then_inc(s_heads, 16)
                    sp.dma_start(hw[:, :, P + 2 * LD:], wout).then_inc(s_heads, 16)
                    load_experts(sp, 0)
                    for c in range(GROUPS):
                        sp.wait_ge(route.gate, c + 1)
                        sp.dma_start(by_group(rows_d[0], c), xa_gate[:, c * KB:(c + 1) * KB, :]).then_inc(s_rows[0], 16)
                        if 1 <= c <= ALONE:
                            store_alone(sp, c - 1)
                @block.gpsimd
                def _(pool):
                    pool.memset(ones_f[:], 1.0).then_inc(s_ones, 1)
                    pool.memset(row_bufs[:], 0.0).then_inc(s_ones, 1)
                    pool.wait_ge(s_small, 16 * 8)
                    for i in range(TURNS):
                        for c in groups_due(i, 1):
                            norm.root(pool, c)
                        for c in groups_due(i, 4):
                            if c < ALONE:
                                alone.root(pool, c)

                @block.tensor
                def _(pe):
                    pe.wait_ge(s_first, 48)
                    pe.matmul(psum[:, 7, 0:P], wsm[:, 0, :], wsm[:, 1, :], start=True, stop=True).then_inc(s_qk, 1)
                    for t in range(NT):
                        if t % NS == 0:
                            pe.wait_ge(s_xt[t // NS], 16)
                        mm = pe.matmul(psum[:, t // KB, (t % KB) * D:(t % KB + 1) * D], xt[:, t * P:(t + 1) * P],
                                       wsm[:, 2, :], start=True, stop=True)
                        if t % KB == KB - 1:
                            mm.then_inc(s_v, 1)
                    pe.wait_ge(s_qkc, 1)
                    for c in range(T // 512):
                        pe.matmul(psum[:, 4 + c, :], qk[:], xt[:, c * 512:(c + 1) * 512],
                                  start=True, stop=True).then_inc(s_qt, 1)

                    def scores(i):
                        b, r = divmod(i, NS)
                        if i == 0:
                            pe.wait_ge(s_qtc, T // 512)
                            pe.wait_ge(s_vc, T // 512)
                            pe.wait_ge(s_cb, 1)
                            pe.wait_ge(s_small, 16 * 8)
                        if i >= 2:
                            pe.wait_ge(s_exp, i - 1)
                        w = (r + 1) * P
                        for c in range(0, w, 512):
                            k = min(512, w - c)
                            last = c + k == w
                            dst = psum[:, 2 * (i % 2) + c // 512, 0:k]
                            pe.matmul(dst, qt[:, i * P:(i + 1) * P], xt[:, b * S + c:b * S + c + k],
                                      start=True, stop=not last)
                        pe.matmul(dst[:, k - P:k], ident_b, mask_qk, start=False, stop=True).then_inc(s_sc, 1)

                    def turn(i):
                        r = i % NS
                        pe.wait_ge(s_exp, i + 1)
                        for c in range(r // KB + 1):
                            n = first[i] + c
                            if n >= 2:
                                pe.wait_ge(s_trc, n - 1)
                            for j in range(c * KB, min(r + 1, (c + 1) * KB)):
                                mm = pe.transpose(psum[:, 4 + n % 2, (j % KB) * P:(j % KB + 1) * P],
                                                  prob[:, i % 2, j * P:(j + 1) * P], ident)
                            mm.then_inc(s_tr, 1)

                    def weigh(i):
                        b, r = divmod(i, NS)
                        pe.wait_ge(s_trc, first[i + 1])
                        if i >= 1:
                            pe.wait_ge(norm.pre, i)
                        for j in range(r + 1):
                            mm = pe.matmul(psum[:, 6, 0:D], prob_t[:, i % 2, j, :], v[:, b * NS + j, :],
                                           start=(j == 0), stop=(j == r))
                        mm.then_inc(s_o, 1)

                    def head_queries():
                        pe.wait_ge(s_heads, 64)
                        pe.wait_ge(s_exp, NT)
                        for h in range(H):
                            mm = pe.matmul(psum[:, 0, h * LD:(h + 1) * LD], hw[:, h, 0:P], hw[:, h, P:P + LD],
                                           start=True, stop=True)
                        mm.then_inc(s_hq, 1)

                    scores(0)
                    for i in range(TURNS):
                        if i + 1 < NT:
                            scores(i + 1)
                        if 1 <= i <= NT:
                            weigh(i - 1)
                        if i < NT:
                            turn(i)
                        for c in groups_due(i, 3):
                            route.turn(pe, c)
                        for c in groups_due(i, 4):
                            route.logits(pe, c)
                        for c in groups_due(i, 5):
                            route.tally(pe, c)
                        if i == NT:
                            head_queries()
                    route.sum_table(pe)

                @block.scalar
                def _(act):
                    act.dma_start(wsm[:, 2, :], wv0_t).then_inc(s_first, 16)
                    act.dma_start(cb_f[:], const_b_d).then_inc(s_cb_in, 16)
                    act.dma_start(cf[:], const_f_d).then_inc(s_small, 16)
                    act.dma_start(rt[:, 0, :], router).then_inc(s_small, 16)
                    act.dma_start(rt[:, 1, :], gate_w_t).then_inc(s_small, 16)
                    act.dma_start(gb[:], gate_b.rearrange("(o e) -> o e", o=1)).then_inc(s_small, 16)
                    act.wait_ge(s_cb_in, 16)
                    nc.scalar.copy(cb[:], cb_f[:]).then_inc(s_cb, 1)
                    for c in range(T // 512):
                        act.wait_ge(s_v, c + 1)
                        nc.scalar.copy(v[:, c * KB:(c + 1) * KB, :],
                                       psum[:, c, :].rearrange("p (t d) -> p t d", d=D)).then_inc(s_vc, 1)
                    def exponentials(i):
                        w = (i % NS + 1) * P
                        act.wait_ge(s_nm, i + 1)
                        if i >= 2:
                            act.wait_ge(s_tr, first[i - 1])
                        nc.scalar.activation(prob[:, i % 2, 0:w],
                                             psum[:, 2 * (i % 2):2 * (i % 2) + 2, :].rearrange("p a n -> p (a n)")[:, 0:w],
                                             ACT.Exp, bias=nm[:, i:i + 1], scale=SCALE0,
                                             accum_out=den[:, i:i + 1]).then_inc(s_exp, 1)

                    def copy_turned(i):
                        r = i % NS
                        for c in range(r // KB + 1):
                            n = first[i] + c
                            k = min(KB, r + 1 - c * KB)
                            act.wait_ge(s_tr, n + 1)
                            if i >= 2 and c == 0:
                                act.wait_ge(s_o, i - 1)
                            nc.scalar.copy(prob_t[:, i % 2, c * KB:c * KB + k, :],
                                           psum[:, 4 + n % 2, 0:k * P].rearrange("p (j q) -> p j q", q=P)
                                           ).then_inc(s_trc, 1)

                    exponentials(0)
                    for i in range(TURNS):
                        if i < NT:
                            copy_turned(i)
                        if i + 1 < NT:
                            exponentials(i + 1)
                        for c in groups_due(i, 3):
                            route.copy(act, c)
                        for c in groups_due(i, 4):
                            route.exp(act, c)
                        if i == NT + 2:
                            act.wait_ge(s_hq, 1)
                            nc.scalar.copy(wqk[:], psum[:, 0, :]).then_inc(s_hqc, 1)

                @block.vector
                def _(dve):
                    dve.wait_ge(s_qk, 1)
                    dve.tensor_copy(qk[:], psum[:, 7, 0:P]).then_inc(s_qkc, 1)
                    for c in range(T // 512):
                        dve.wait_ge(s_qt, c + 1)
                        dve.tensor_copy(qt[:, c * 512:(c + 1) * 512], psum[:, 4 + c, :]).then_inc(s_qtc, 1)

                    def row_max(i):
                        w = (i % NS + 1) * P
                        dve.wait_ge(s_sc, i + 1)
                        dve.tensor_reduce(m[:, i:i + 1], psum[:, 2 * (i % 2):2 * (i % 2) + 2, :].rearrange(
                            "p a n -> p (a n)")[:, 0:w], AX.X, ALU.max).then_inc(s_m, 1)
                        dve.wait_ge(s_m, i + 1)
                        dve.tensor_scalar(nm[:, i:i + 1], m[:, i:i + 1], -SCALE0, None, ALU.mult).then_inc(s_nm, 1)

                    def take(i):
                        dve.wait_ge(s_exp, i + 1)
                        dve.reciprocal(rden[:, i:i + 1], den[:, i:i + 1]).then_inc(s_rd, 1)
                        dve.wait_ge(s_rd, i + 1)
                        dve.wait_ge(s_o, i + 1)
                        dve.scalar_tensor_tensor(pre[:, i, :], psum[:, 6, 0:D], rden[:, i:i + 1],
                                                 x0[:, i, :], ALU.mult, ALU.add).then_inc(norm.pre, 1)
                        norm.take(dve, i)

                    row_max(0)
                    dve.wait_ge(s_x, 16)
                    dve.wait_ge(s_small, 16 * 8)
                    for i in range(TURNS):
                        if i + 1 < NT:
                            row_max(i + 1)
                        if 1 <= i <= NT:
                            take(i - 1)
                        for c in groups_due(i, 5):
                            if c < ALONE:
                                alone.apply(dve, c)
                        for c in groups_due(i, 2):
                            if c < GROUPS - 1:
                                norm.apply(dve, c)
                        if i == NT:
                            norm.apply(dve, GROUPS - 1)
                        for c in groups_due(i, 4):
                            route.choose(dve, c)
                        for c in groups_due(i, 5):
                            route.settle(dve, c)
                        for c in groups_due(i, 3):
                            if c < ALONE:
                                for t in range(c * KB, (c + 1) * KB):
                                    alone.take(dve, t)
                    route.take_table(dve)

        def experts(layer, dst_d):
            tiles = TILES[layer]
            route = routes[layer]
            UN = 4
            W = (D + 1, D)[layer]
            c3 = ExitStack()
            with c3, nc.Block() as block:
                def sb3(name, shape, dt=F32):
                    return c3.enter_context(nc.sbuf_tensor(f"f{layer}_{name}", shape, dt))

                def sm(name):
                    return sem(f"f{layer}_{name}")

                rows = row_bufs[:, :, 0:W]
                rows_t = sb3("rows_t", [P, 2, P])
                keep = sb3("keep", [P, UN, W])
                w1_now = sb3("w1_now", [P, UN, W1])
                hid = sb3("hid", [P, 2, FC, P])
                summed = sb3("summed", [P, UN, D])
                normed = sb3("normed", [P, UN, D])
                bn = sb3("bn", [P, UN, 6])
                mean = sb3("mean", [P, UN, 2])
                var_e = sb3("var_e", [P, UN])
                root = sb3("root", [P, UN])
                idx_in = sb3("idx_in", [P, UN], I32)
                idx_out = sb3("idx_out", [P, UN], I32)
                s_in = [sm(f"rows_in{w}") for w in range(UN)]
                s_out = [sm(f"scattered{w}") for w in range(UN)]
                (s_ix, s_keep, s_tr, s_trc, s_w1, s_h, s_ra, s_rb, s_y, s_pre, s_bn, s_st, s_var, s_root, s_norm) = (
                    sm(n) for n in (
                        "index_in", "row_kept", "row_turned", "row_copied", "w1_chosen", "hidden", "relu_act",
                        "relu_dve", "out", "summed", "bn", "stats", "var", "root", "normed"))


                if layer == 0:
                    s_hw = sm("head_outputs")

                def there(t):
                    return not isinstance(t, int) or t < tiles

                def later(t, n):
                    return not isinstance(t, int) or t >= n

                def nth_of(t, k, off):
                    return t // UN if k is None else k + off // UN

                def expert_of(eng, t, k, off):
                    if layer == 0:
                        return t * P // CAP if k is None else (UN * P // CAP) * k + (off * P) // CAP
                    at = owner[0:1, t:t + 1] if k is None else owner[0:1, bass.ds(UN * k + off, 1)]
                    return eng.value_load(at, min_val=0, max_val=E - 1)

                def over_tiles(eng, body):
                    stop = UN * ((tiles - 4) // UN)
                    for t in range(UN):
                        body(t, None, t)
                    with eng.Fori(1, stop // UN) as k:
                        for w in range(UN):
                            body(UN * k + w, k, w)
                    for t in range(stop, tiles):
                        body(t, None, t)

                @block.gpsimd
                def _(pool):
                    last_token = pool.to_reg(T - 1)

                    def gather(w):
                        pool.indirect_dma_start(
                            rows[:, w, :], None, rows_d[layer], bass.IndirectOffsetOnAxis(ap=idx_in[:, w:w + 1], axis=0),
                            bounds_check=last_token, oob_is_err=False).then_inc(s_in[w], 16)

                    def scatter(w):
                        pool.indirect_dma_start(
                            dst_d, bass.IndirectOffsetOnAxis(ap=idx_out[:, w:w + 1], axis=0), normed[:, w, :], None,
                            bounds_check=last_token, oob_is_err=False).then_inc(s_out[w], 16)

                    pool.wait_ge(s_rows[layer], 16 * GROUPS)
                    pool.wait_ge(s_ix, UN)
                    for t in range(UN):
                        gather(t)
                    if layer == 0:
                        for c in range(ALONE, GROUPS):
                            alone.root(pool, c)

                    def take_root(t, w):
                        pool.wait_ge(s_var, t + 1)
                        pool.tensor_tensor(root[:, w:w + 1], var_e[:, w:w + 1], half[:, 0:1], ALU.pow
                                           ).then_inc(s_root, 1)

                    def step(t, k, off):
                        w = off % UN
                        if later(t, 1):
                            if there(t + UN):
                                pool.wait_ge(s_ix, t + UN + 1)
                                pool.wait_ge(s_keep, t + 1)
                            if later(t, 2):
                                pool.wait_ge(s_norm, t - 1)
                            take_root(t - 1, (w - 1) % UN)
                        else:
                            pool.wait_ge(s_ix, UN + 1)
                            pool.wait_ge(s_keep, 1)
                        if there(t + UN):
                            gather(w)
                        if layer == 0 and k is None and t == 2:
                            pool.wait_ge(s_alone, 16 * GROUPS)
                        if later(t, 2):
                            scatter((w - 2) % UN)
                    over_tiles(pool, step)
                    pool.wait_ge(s_norm, tiles - 1)
                    take_root(tiles - 1, (tiles - 1) % UN)
                    scatter((tiles - 2) % UN)
                    pool.wait_ge(s_norm, tiles)
                    scatter((tiles - 1) % UN)
                    for w in range(UN):
                        pool.wait_ge(s_out[w], 16 * len(range(w, tiles, UN)))

                if layer == 0:
                    @block.sync
                    def _(sp):
                        for c in range(ALONE, GROUPS):
                            store_alone(sp, c)

                @block.tensor
                def _(pe):
                    pe.wait_ge(s_w[layer], EXPERT_LOADS)

                    def turn(t, k, off):
                        pe.wait_ge(s_in[off % UN], 16 * (nth_of(t, k, off) + 1))
                        if later(t, 2):
                            pe.wait_ge(s_trc, t - 1)
                        pe.transpose(psum[:, off % 2, 0:P], rows[:, off % UN, 0:D], ident).then_inc(s_tr, 1)

                    def hidden(t, k, off):
                        par = off % 2
                        pe.wait_ge(s_trc, t + 1)
                        pe.wait_ge(s_w1, t + 1)
                        if later(t, 2):
                            pe.wait_ge(s_ra, t - 1)
                            pe.wait_ge(s_rb, t - 1)
                        for c in range(FC):
                            mm = pe.matmul(psum[:, 2 + 2 * par + c % 2, (c // 2) * P:(c // 2 + 1) * P],
                                           w1_now[:, off % UN, c * P:(c + 1) * P], rows_t[:, par, :],
                                           start=True, stop=True)
                        mm.then_inc(s_h, 1)

                    def out(t, k, off):
                        par = off % 2
                        e = expert_of(pe, t, k, off)
                        pe.wait_ge(s_ra, t + 1)
                        pe.wait_ge(s_rb, t + 1)
                        if later(t, 2):
                            pe.wait_ge(s_pre, t - 1)
                        dst_y = psum[:, 6 + par, 0:D]
                        for c in range(FC):
                            pe.matmul(dst_y, hid[:, par, c, :], w2[:, bass.ds(e, 1), c, :],
                                      start=(c == 0), stop=False)
                        mm = pe.matmul(dst_y, ones_f[:], b2[0:1, bass.ds(e, 1), :], start=False, stop=True)
                        mm.then_inc(s_y, 1)

                    turn(0, None, 0)
                    turn(1, None, 1)
                    hidden(0, None, 0)

                    def step(t, k, off):
                        if there(t + 1):
                            hidden(t + 1, k, off + 1)
                        if there(t + 2):
                            turn(t + 2, k, off + 2)
                        out(t, k, off)
                    over_tiles(pe, step)
                    if layer == 0:
                        for h in range(H):
                            o = (h % HG) * LD
                            mm = pe.matmul(psum[o:o + LD, 0, (h // HG) * D:(h // HG + 1) * D],
                                           hw[:, h, P + LD:P + 2 * LD], hw[:, h, P + 2 * LD:], start=True, stop=True)
                        mm.then_inc(s_hw, 1)

                @block.scalar
                def _(act):
                    def copy_rows(t, k, off):
                        act.wait_ge(s_tr, t + 1)
                        if later(t, 2):
                            act.wait_ge(s_h, t - 1)
                        nc.scalar.copy(rows_t[:, off % 2, :], psum[:, off % 2, 0:P]).then_inc(s_trc, 1)
                        if later(t, UN):
                            act.wait_ge(s_pre, t - UN + 1)
                        nc.scalar.copy(keep[:, off % UN, :], rows[:, off % UN, :]).then_inc(s_keep, 1)

                    def choose(t, k, off):
                        e = expert_of(act, t, k, off)
                        nc.scalar.copy(w1_now[:, off % UN:off % UN + 1, :], w1[:, bass.ds(e, 1), :]).then_inc(s_w1, 1)

                    def relu(t, k, off):
                        par = off % 2
                        if later(t, 2):
                            act.wait_ge(s_ra, t - 1)
                            act.wait_ge(s_rb, t - 1)
                        act.wait_ge(s_h, t + 1)
                        if later(t, 2):
                            act.wait_ge(s_y, t - 1)
                        for c in (0, 2):
                            ins = nc.scalar.activation(hid[:, par, c, :],
                                                       psum[:, 2 + 2 * par, (c // 2) * P:(c // 2 + 1) * P],
                                                       ACT.Relu, bias=w1_now[:, off % UN, F + c:F + c + 1])
                        ins.then_inc(s_ra, 1)

                    act.wait_ge(s_w[layer], EXPERT_LOADS)
                    choose(0, None, 0)
                    choose(1, None, 1)
                    choose(2, None, 2)
                    copy_rows(0, None, 0)
                    copy_rows(1, None, 1)
                    relu(0, None, 0)

                    def step(t, k, off):
                        if there(t + 1):
                            relu(t + 1, k, off + 1)
                        if there(t + 2):
                            copy_rows(t + 2, k, off + 2)
                        if there(t + 3):
                            choose(t + 3, k, off + 3)
                    over_tiles(act, step)
                    if layer == 0:
                        act.wait_ge(s_hw, 1)
                        nc.scalar.copy(wvo[:], psum[:, 0, :].rearrange("p (g d) -> p g d", d=D))

                @block.vector
                def _(dve):
                    def relu(t, k, off):
                        par = off % 2
                        dve.wait_ge(s_h, t + 1)
                        if later(t, 2):
                            dve.wait_ge(s_y, t - 1)
                        for c in (1, 3):
                            ins = dve.tensor_scalar(hid[:, par, c, :],
                                                    psum[:, 3 + 2 * par, (c // 2) * P:(c // 2 + 1) * P],
                                                    w1_now[:, off % UN, F + c:F + c + 1], 0.0, ALU.add, ALU.max)
                        ins.then_inc(s_rb, 1)

                    def column(k, off):
                        return table[:, off:off + 1] if k is None else table[:, bass.ds(UN * k + off, 1)]

                    def index_in(t, k, off):
                        if later(t, UN):
                            dve.wait_ge(s_tr, t - UN + 1)
                        dve.tensor_scalar(idx_in[:, off % UN:off % UN + 1], column(k, off), 1.0, None, ALU.mult
                                          ).then_inc(s_ix, 1)

                    def add_up(t, k, off):
                        w = off % UN
                        y = psum[:, 6 + off % 2, 0:D]
                        if later(t, UN):
                            dve.wait_ge(s_out[w], 16 * nth_of(t, k, off))
                        dve.wait_ge(s_keep, t + 1)
                        dve.wait_ge(s_y, t + 1)
                        if layer == 0:
                            dve.scalar_tensor_tensor(summed[:, w, :], y, keep[:, w, D:D + 1], keep[:, w, 0:D],
                                                     ALU.mult, ALU.add).then_inc(s_pre, 1)
                        else:
                            dve.tensor_tensor(summed[:, w, :], y, keep[:, w, :], ALU.add).then_inc(s_pre, 1)
                        dve.wait_ge(s_pre, t + 1)
                        dve.bn_stats(bn[:, w, :], summed[:, w, :]).then_inc(s_bn, 1)
                        dve.wait_ge(s_bn, t + 1)
                        dve.tensor_scalar(idx_out[:, w:w + 1], column(k, off), 1.0, None, ALU.mult)
                        dve.bn_aggr(mean[:, w, :], bn[:, w, :]).then_inc(s_st, 1)
                        dve.wait_ge(s_st, t + 1)
                        dve.tensor_scalar(var_e[:, w:w + 1], mean[:, w, 1:2], EPS, None, ALU.add).then_inc(s_var, 1)

                    def apply(t, k, off):
                        w = off % UN
                        dve.wait_ge(s_root, t + 1)
                        dve.tensor_scalar(normed[:, w, :], summed[:, w, :], mean[:, w, 0:1], root[:, w:w + 1],
                                          ALU.subtract, ALU.mult).then_inc(s_norm, 1)

                    dve.wait_ge(route.table, 1)
                    for t in range(4):
                        index_in(t, None, t)
                    if layer == 0:
                        for t in range(ALONE * KB, NT):
                            alone.take(dve, t)
                    if layer == 0:
                        for c in range(ALONE, GROUPS):
                            alone.apply(dve, c)
                    relu(0, None, 0)

                    def step(t, k, off):
                        if there(t + UN):
                            index_in(t + UN, k, off + UN)
                        if there(t + 1):
                            relu(t + 1, k, off + 1)
                        if later(t, 1):
                            apply(t - 1, k, off - 1)
                        add_up(t, k, off)
                    over_tiles(dve, step)
                    apply(tiles - 1, None, tiles - 1)

        def attend1(src, dst):
            c2 = ExitStack()
            with c2:
                def sb2(name, shape, dt=F32):
                    return c2.enter_context(nc.sbuf_tensor("a1_" + name, shape, dt))

                def sm(name):
                    return sem("a1_" + name)

                lat = sb2("lat", [P, T], F16)
                latv = sb2("latv", [P, NT, 2 * LD + 2], F16)
                Y1 = 2 * LD + 1
                U = H * B
                UN = 4
                q = sb2("q", [P, UN, S], F16)
                nmax = sb2("nmax", [P, UN, 2 * NS])
                diag = sb2("diag", [P, UN, NS, P], BF16)
                s_q = [sm(f"q_in{w}") for w in range(UN)]
                s_st = [sm("q_stored_a"), sm("q_stored_b")]

                def load_queries(sp, w, h):
                    b = w % B
                    for r in range(4):
                        sp.dma_start(q[r * LD:(r + 1) * LD, w, :],
                                     q_d[r // 2][bass.ds(h * LD, LD), b * S:(b + 1) * S]).then_inc(s_q[w], 16)

                with ExitStack() as c3, nc.Block() as block:
                    GC = KB * P
                    qh = c3.enter_context(nc.sbuf_tensor("a1_qh", [P, 2, G, GC], F16))
                    ql = c3.enter_context(nc.sbuf_tensor("a1_ql", [P, 2, G, GC], F16))
                    s_tr, s_trc, s_p, s_ph, s_pl, s_v, s_vh, s_vl, s_one = (sm(n) for n in (
                        "turned", "turned_copied", "projected", "high", "low", "latv", "latv_high", "latv_low", "ones"))
                    s_got = [sm(f"fetched{c}") for c in range(GROUPS)]
                    NJ = G + 1

                    @block.gpsimd
                    def _(pool):
                        pool.memset(latv[:, :, 2 * LD:2 * LD + 2], 1.0).then_inc(s_one, 1)

                    @block.tensor
                    def _(pe):
                        def turn(c):
                            pe.wait_ge(s_got[c], 16)
                            if c >= 2:
                                pe.wait_ge(s_trc, c - 1)
                            for t in range(KB):
                                mm = pe.transpose(psum[:, c % 2, t * P:(t + 1) * P], src[:, c * KB + t, :], ident)
                            mm.then_inc(s_tr, 1)

                        turn(0)
                        for c in range(GROUPS):
                            cols = slice(c * GC, (c + 1) * GC)
                            if c + 1 < GROUPS:
                                turn(c + 1)
                            pe.wait_ge(s_trc, c + 1)
                            for j in range(NJ):
                                n = NJ * c + j
                                if n >= 4:
                                    pe.wait_ge(s_pl, n - 3)
                                w = wkv_s[:].rearrange("p r c -> p (r c)") if j == 0 else wqk[:, (j - 1) * P:j * P]
                                pe.matmul(psum[:, 2 + n % 4, :], w, xt[:, cols], start=True, stop=True).then_inc(s_p, 1)
                            if c >= 2:
                                pe.wait_ge(s_vl, c - 1)
                            for t in range(KB):
                                mm = pe.matmul(psum[:, 6 + c % 2, t * LD:(t + 1) * LD],
                                               xt[:, (c * KB + t) * P:(c * KB + t + 1) * P], wkv_s[:, 0, :],
                                               start=True, stop=True)
                            mm.then_inc(s_v, 1)

                    def by_token(c):
                        return (latv[:, c * KB:(c + 1) * KB, :],
                                psum[:, 6 + c % 2, 0:KB * LD].rearrange("p (t c) -> p t c", c=LD))

                    @block.scalar
                    def _(act):
                        def copy_turned(c):
                            act.wait_ge(s_tr, c + 1)
                            nc.scalar.copy(xt[:, c * GC:(c + 1) * GC], psum[:, c % 2, :]).then_inc(s_trc, 1)

                        copy_turned(0)
                        for c in range(GROUPS):
                            cols = slice(c * GC, (c + 1) * GC)
                            for j in range(NJ):
                                n = NJ * c + j
                                act.wait_ge(s_p, n + 1)
                                if c >= 2 and j == 1:
                                    act.wait_ge(s_st[c % 2], 32 * (c // 2))
                                hi = lat[:, cols] if j == 0 else qh[:, c % 2, j - 1, :]
                                nc.scalar.copy(hi, psum[:, 2 + n % 4, :]).then_inc(s_ph, 1)
                                if j == 0 and c + 1 < GROUPS:
                                    copy_turned(c + 1)
                            act.wait_ge(s_v, c + 1)
                            hi, ps = by_token(c)
                            nc.scalar.copy(hi[:, :, 0:LD], ps).then_inc(s_vh, 1)

                    @block.vector
                    def _(dve):
                        def split(c):
                            cols = slice(c * GC, (c + 1) * GC)
                            for j in range(NJ):
                                n = NJ * c + j
                                dve.wait_ge(s_ph, n + 1)
                                if j == 0:
                                    for r in (1, 3):
                                        rs = slice(r * LD, (r + 1) * LD)
                                        ins = dve.tensor_tensor(lat[rs, cols], psum[rs, 2 + n % 4, :], lat[rs, cols],
                                                                ALU.subtract)
                                else:
                                    if c >= 2 and j == 1:
                                        dve.wait_ge(s_st[c % 2], 32 * (c // 2))
                                    ins = dve.tensor_tensor(ql[:, c % 2, j - 1, :], psum[:, 2 + n % 4, :],
                                                            qh[:, c % 2, j - 1, :], ALU.subtract)
                                ins.then_inc(s_pl, 1)
                            dve.wait_ge(s_vh, c + 1)
                            hi, ps = by_token(c)
                            dve.tensor_tensor(hi[:, :, LD:2 * LD], ps, hi[:, :, 0:LD], ALU.subtract).then_inc(s_vl, 1)

                        for c in range(GROUPS):
                            split(c)

                    @block.sync
                    def _(sp):
                        for c in range(GROUPS):
                            sp.dma_start(src[:, c * KB:(c + 1) * KB, :], by_group(x2_d, c)).then_inc(s_got[c], 16)
                        for c in range(GROUPS):
                            sp.wait_ge(s_pl, NJ * (c + 1))
                            for part, parts in enumerate((qh, ql)):
                                sp.dma_start(q_d[part].rearrange("(g p) t -> p g t", p=P)[:, :, c * GC:(c + 1) * GC],
                                             parts[:, c % 2]).then_inc(s_st[c % 2], 16)
                            if c == GROUPS // B - 1:
                                for s in s_st:
                                    sp.wait_ge(s, 16 * GROUPS // B)
                                for w in range(0, UN, B):
                                    load_queries(sp, w, w // B)

                with ExitStack() as c3, nc.Block() as block:
                    def sb3(name, shape, dt=F32):
                        return c3.enter_context(nc.sbuf_tensor("a1_" + name, shape, dt))

                    NE = 5
                    LAG = 3
                    ex = sb3("ex", [P, NE, S])
                    ex_h = sb3("ex_h", [P, NE, S], F16)
                    ex_l = sb3("ex_l", [P, NE, S], F16)
                    rden = sb3("rden", [P, NS])
                    sums = sb3("sums", [P, 2, NS, Y1])
                    whole = sb3("whole", [P, NS, LD])
                    s_ms, s_mt, s_nm, s_dg, s_sc, s_ex, s_ld, s_lp, s_pv, s_sm, s_rd, s_wh, s_y = (sm(n) for n in (
                        "max_scored", "max_taken", "max_ready", "diag", "scored", "exp", "low_dve", "low_pool",
                        "weighed", "sums", "recip", "whole", "y"))
                    pieces = [(i, c, min(512, (i + 1) * P - c)) for i in range(NS) for c in range(0, (i + 1) * P, 512)]
                    NP = len(pieces)
                    groups = [(0,)] + [(j, NS - j) for j in range(1, NS // 2)] + [(NS // 2,)]
                    NG = len(groups)
                    width = [sum(S - j * P for j in g) for g in groups]
                    share = [0] + [(g + 1) * NP // NG for g in range(NG)]

                    def over_units(eng, body):
                        for u in range(UN):
                            body(u, u, u // B)
                        with eng.Fori(1, U // UN - 1) as k:
                            for w in range(UN):
                                body(UN * k + w, w, (UN // B) * k + w // B)
                        for u in range(U - UN, U):
                            body(u, u % UN, u // B)

                    def early(u, n):
                        return isinstance(u, int) and u < n

                    def ending(u, n):
                        return isinstance(u, int) and u + n >= U

                    @block.sync
                    def _(sp):
                        for s in s_st:
                            sp.wait_ge(s, 16 * GROUPS)
                        def load(u, w, h):
                            if not early(u, UN):
                                sp.wait_ge(s_sc, NG * (u - UN + 1))
                            if not (early(u, UN) and u % B == 0):
                                load_queries(sp, w, h)
                            if isinstance(u, int) and u == UN - 1:
                                load_experts(sp, 1)
                        over_units(sp, load)

                    @block.tensor
                    def _(pe):
                        def max_piece(u, w, turns, n):
                            i, c, wd = pieces[n]
                            if n == 0:
                                pe.wait_ge(s_q[w], 64 * turns)
                            if not (early(u, 1) and n < 2):
                                pe.wait_ge(s_mt, NP * u + n - 1)
                            b = w % B
                            done = c + wd == (i + 1) * P
                            dst_s = psum[:, n % 2, 0:wd]
                            mm = pe.matmul(dst_s, q[:, w, i * P:(i + 1) * P], lat[:, b * S + c:b * S + c + wd],
                                           start=True, stop=not done)
                            if done:
                                mm = pe.matmul(dst_s[:, wd - P:wd], ident_b, mask_qk, start=False, stop=True)
                            mm.then_inc(s_ms, 1)

                        def score(u, w, g, bank):
                            b = w % B
                            if g == 0 and bank == 0:
                                pe.wait_ge(s_dg, NS * (u + 1))
                            if bank == 0 and not (early(u, 1) and g < 2):
                                pe.wait_ge(s_ex, NG * u + g - 1)
                            at = 0
                            for j in groups[g]:
                                lo = j * P
                                while lo < S:
                                    k = min(S - lo, 512 - at % 512)
                                    if at // 512 != bank:
                                        lo, at = lo + k, at + k
                                        continue
                                    dst_s = psum[:, 2 + 2 * ((NG * w + g) % 2) + at // 512, at % 512:at % 512 + k]
                                    pe.matmul(dst_s, lat[:, b * S + j * P:b * S + (j + 1) * P], q[:, w, lo:lo + k],
                                              start=True, stop=False)
                                    diagonal = lo == j * P
                                    mm = pe.matmul(dst_s, ones_b,
                                                   diag[:, w, lo // P:(lo + k) // P, :].rearrange("p a n -> p (a n)"),
                                                   start=False, stop=not diagonal)
                                    if diagonal:
                                        mm = pe.matmul(dst_s[:, 0:P], ident_b, mask_kq, start=False, stop=True)
                                    lo, at = lo + k, at + k
                            if bank == (width[g] - 1) // 512:
                                mm.then_inc(s_sc, 1)

                        def weigh(u, w, g, part_of_two):
                            b = w % B
                            if part_of_two == 1:
                                pass
                            elif g == NG - 1:
                                pe.wait_ge(s_ld, u + 1)
                            else:
                                pe.wait_ge(s_lp, (NG - 1) * u + g + 1)
                                if g == 0 and not early(u, 1):
                                    pe.wait_ge(s_sm, u)
                            blocks = [(j, i) for j in groups[g] for i in range(j, NS)]
                            half = len(blocks) // 2
                            for n in range(part_of_two * half, part_of_two * half + half):
                                j, i = blocks[n]
                                for part, e in enumerate((ex_h, ex_l)):
                                    mm = pe.matmul(psum[:, 6 + i // 4, (i % 4) * Y1:(i % 4 + 1) * Y1],
                                                   e[:, (NG * w + g) % NE, n * P:(n + 1) * P], latv[:, b * NS + j, 0:Y1],
                                                   start=(j == 0 and i % 4 == 0 and part == 0),
                                                   stop=(j == i and part == 1), skip_group_check=True)
                            if part_of_two == 1:
                                mm.then_inc(s_pv, 1)

                        for u in range(2):
                            for n in range(NP):
                                max_piece(u, u, 1, n)

                        def unit(u, w, k):
                            for g in range(NG):
                                todo = [] if ending(u, 2) else list(range(share[g], share[g + 1]))

                                def some_max(last=False):
                                    while todo:
                                        max_piece(u + 2, (w + 2) % UN, k + 1 + (w + 2) // UN, todo.pop(0))
                                        if not last:
                                            break

                                def some_weigh(part_of_two):
                                    if g >= LAG:
                                        weigh(u, w, g - LAG, part_of_two)
                                    elif not early(u, 1):
                                        weigh(u - 1, (w - 1) % UN, g - LAG + NG, part_of_two)

                                score(u, w, g, 0)
                                some_max()
                                if width[g] > 512:
                                    score(u, w, g, 1)
                                    some_max()
                                some_weigh(0)
                                some_max(last=True)
                                some_weigh(1)

                        for u in range(UN):
                            unit(u, u, 0)
                        with pe.Fori(1, U // UN - 1) as k:
                            for w in range(UN):
                                unit(UN * k + w, w, k)
                        for u in range(U - UN, U):
                            unit(u, u % UN, u // UN)
                        for g in range(NG - LAG, NG):
                            weigh(U - 1, UN - 1, g, 0)
                            weigh(U - 1, UN - 1, g, 1)

                    @block.scalar
                    def _(act):
                        def copy_sums(u, b):
                            if not early(u, 2):
                                act.wait_ge(s_y, u - 1)
                            act.wait_ge(s_pv, NG * (u + 1))
                            nc.scalar.copy(sums[:, b].rearrange("p (a i) c -> p a (i c)", a=2),
                                           psum[:, 6:8, 0:4 * Y1]).then_inc(s_sm, 1)

                        def unit(u, w, h):
                            for g in range(NG):
                                n = NG * w + g
                                wd = width[g]
                                scores = psum[:, 2 + 2 * (n % 2):4 + 2 * (n % 2), :].rearrange("p a n -> p (a n)")[:, 0:wd]
                                if not (early(u, 1) and g < NE):
                                    act.wait_ge(s_pv, NG * u + g - NE + 1)
                                act.wait_ge(s_sc, NG * u + g + 1)
                                nc.scalar.activation(ex[:, n % NE, 0:wd], scores, ACT.Exp, scale=SCALE1)
                                if g == LAG - 1 and not early(u, 1):
                                    copy_sums(u - 1, (w - 1) % B)
                                nc.scalar.activation(ex_h[:, n % NE, 0:wd], scores, ACT.Exp,
                                                     scale=SCALE1).then_inc(s_ex, 1)
                        for s in s_st:
                            act.wait_ge(s, 16 * GROUPS)
                        over_units(act, unit)
                        copy_sums(U - 1, B - 1)

                    def low_part(eng, w, g):
                        n = (NG * w + g) % NE
                        return eng.tensor_tensor(ex_l[:, n, 0:width[g]], ex[:, n, 0:width[g]], ex_h[:, n, 0:width[g]],
                                                 ALU.subtract)

                    @block.vector
                    def _(dve):
                        def maximum(u, w, n):
                            i, c, wd = pieces[n]
                            if n == 0 and not early(u, UN):
                                dve.wait_ge(s_dg, NS * (u - UN + 1))
                            dve.wait_ge(s_ms, NP * u + n + 1)
                            dve.tensor_reduce(nmax[:, w, i + NS * (c // 512):i + NS * (c // 512) + 1],
                                              psum[:, n % 2, 0:wd], AX.X, ALU.max, negate=True).then_inc(s_mt, 1)
                            if n == NP - 1:
                                dve.wait_ge(s_mt, NP * (u + 1))
                                two = NS // 2
                                dve.tensor_tensor(nmax[:, w, two:NS], nmax[:, w, two:NS],
                                                  nmax[:, w, NS + two:2 * NS], ALU.min).then_inc(s_nm, 1)

                        def diagonal(u, w, i):
                            if i == 0:
                                dve.wait_ge(s_nm, u + 1)
                                if not early(u, UN):
                                    dve.wait_ge(s_sc, NG * (u - UN + 1))
                            dve.tensor_scalar(diag[:, w, i, :], ident_b, nmax[:, w, i:i + 1], None,
                                              ALU.mult).then_inc(s_dg, 1)

                        def last_low(u, w):
                            dve.wait_ge(s_ex, NG * (u + 1))
                            low_part(dve, w, NG - 1).then_inc(s_ld, 1)

                        def output_whole(u, b):
                            dve.wait_ge(s_sm, u + 1)
                            dve.tensor_tensor(whole[:], sums[:, b, :, 0:LD], sums[:, b, :, LD:2 * LD], ALU.add
                                              ).then_inc(s_wh, 1)

                        def output_recip(u, b):
                            dve.reciprocal(rden[:], sums[:, b, :, 2 * LD]).then_inc(s_rd, 1)

                        def output_scaled(u, b, h):
                            dve.wait_ge(s_wh, u + 1)
                            dve.wait_ge(s_rd, u + 1)
                            dve.tensor_tensor(y_all[:, b * NS:(b + 1) * NS, bass.ds(h * LD, LD)], whole[:],
                                              rden[:].unsqueeze(2).broadcast_to((P, NS, LD)), ALU.mult).then_inc(s_y, 1)

                        for u in range(2):
                            for n in range(NP):
                                maximum(u, u, n)
                        for i in range(NS):
                            diagonal(0, 0, i)

                        def unit(u, w, h):
                            for n in range(NP):
                                if not ending(u, 2):
                                    maximum(u + 2, (w + 2) % UN, n)
                                if n < NS and not ending(u, 1):
                                    diagonal(u + 1, (w + 1) % UN, n)
                                if not early(u, 1):
                                    if n == 1:
                                        last_low(u - 1, (w - 1) % UN)
                                    if n == NP - 3:
                                        output_whole(u - 1, (w - 1) % B)
                                    if n == NP - 2:
                                        output_recip(u - 1, (w - 1) % B)
                                    if n == NP - 1:
                                        output_scaled(u - 1, (w - 1) % B, h if w % B else h - 1)
                        over_units(dve, unit)
                        last_low(U - 1, UN - 1)
                        output_whole(U - 1, B - 1)
                        output_recip(U - 1, B - 1)
                        output_scaled(U - 1, B - 1, H - 1)

                    @block.gpsimd
                    def _(pool):
                        def unit(u, w, h):
                            for g in range(NG - 1):
                                pool.wait_ge(s_ex, NG * u + g + 1)
                                low_part(pool, w, g).then_inc(s_lp, 1)
                        over_units(pool, unit)

                with ExitStack() as c3, nc.Block() as block:
                    yt = c3.enter_context(nc.sbuf_tensor("a1_yt", [P, 2, G, P], F32))
                    s_tr, s_trc, s_o = (sm("o_" + n) for n in ("turned", "copied", "out"))
                    norm, route = norm2, route1
                    TURNS = NT + 9

                    @block.tensor
                    def _(pe):
                        def turn(t):
                            if t >= 2:
                                pe.wait_ge(s_trc, t - 1)
                            for g in range(G):
                                mm = pe.transpose(psum[:, t % 2, g * P:(g + 1) * P], y_all[:, t, g * P:(g + 1) * P], ident)
                            mm.then_inc(s_tr, 1)
                        turn(0)
                        for t in range(TURNS):
                            if t + 1 < NT:
                                turn(t + 1)
                            if t < NT:
                                pe.wait_ge(s_trc, t + 1)
                                if t >= 2:
                                    pe.wait_ge(norm.pre, t - 1)
                                for g in range(G):
                                    mm = pe.matmul(psum[:, 2 + t % 2, 0:D], yt[:, t % 2, g, :], wvo[:, g, :],
                                                   start=(g == 0), stop=(g == G - 1))
                                mm.then_inc(s_o, 1)
                            for c in groups_due(t, 3, 1):
                                route.turn(pe, c)
                            for c in groups_due(t, 4, 1):
                                route.logits(pe, c)
                            for c in groups_due(t, 5, 1):
                                route.tally(pe, c)
                        route.sum_table(pe)

                    @block.sync
                    def _(sp):
                        for c in range(GROUPS):
                            sp.wait_ge(norm.done, KB * (c + 1))
                            sp.dma_start(by_group(rows_d[1], c), dst[:, c * KB:(c + 1) * KB, :]).then_inc(s_rows[1], 16)

                    @block.scalar
                    def _(act):
                        for t in range(TURNS):
                            if t < NT:
                                act.wait_ge(s_tr, t + 1)
                                if t >= 2:
                                    act.wait_ge(s_o, t - 1)
                                nc.scalar.copy(yt[:, t % 2], psum[:, t % 2, :].rearrange("p (g q) -> p g q", q=P)
                                               ).then_inc(s_trc, 1)
                            for c in groups_due(t - 1, 3, 1):
                                route.copy(act, c)

                    @block.vector
                    def _(dve):
                        for t in range(TURNS):
                            if t < NT:
                                dve.wait_ge(s_o, t + 1)
                                dve.tensor_tensor(pre[:, t, :], psum[:, 2 + t % 2, 0:D], src[:, t, :], ALU.add
                                                  ).then_inc(norm.pre, 1)
                                norm.take(dve, t)
                            for c in groups_due(t, 1):
                                if c < GROUPS - 1:
                                    norm.apply(dve, c)
                            for c in groups_due(t, 4, 1):
                                route.choose(dve, c)
                            if t == NT - 1:
                                norm.apply(dve, GROUPS - 1)
                            for c in groups_due(t, 5, 1):
                                route.settle(dve, c)
                        route.settle_all(dve)

                    @block.gpsimd
                    def _(pool):
                        for c in range(GROUPS):
                            norm.root(pool, c)

        attend0()
        experts(0, x2_d)
        attend1(xb, xa)
        experts(1, out_d)


def constants(T, E, tiles):
    import numpy as np
    NT = T // P
    f = np.zeros((P, 4 * P + NT * E + E * NT + E * E), np.float32)
    f[:, 0:P] = np.eye(P)
    f[:, P:P + NT * E] = np.tile(E - np.arange(E), NT)
    f[:, 2 * P:2 * P + E * NT] = np.tile(P * np.arange(NT), E)
    f[:, 3 * P:3 * P + tiles * E] = np.repeat(np.arange(tiles), E)
    at = 3 * P + tiles * E
    f[:, at:at + NT] = -0.5
    f[:, at + NT:at + 2 * NT] = np.arange(NT) - NT
    f[:, at + 2 * NT] = np.arange(P)
    f[:, at + 2 * NT + 1:at + 2 * NT + 1 + E * E] = np.tril(np.ones((E, E)), -1).reshape(-1)
    i = np.arange(P)
    b = np.concatenate([np.eye(P), np.ones((P, P)), (i[:, None] <= i[None, :]),
                        np.where(i[None, :] > i[:, None], NEG, 0.0),
                        np.where(i[:, None] > i[None, :], NEG, 0.0),
                        np.tile(i - (P - 1), (P, 1))], axis=1).astype(np.float32)
    return f, b


def kernel(**inputs):
    import numpy as np
    import concourse.bacc as bacc
    from concourse.bass_utils import run_bass_kernel_spmd

    a = {k: np.asarray(v) for k, v in inputs.items()}
    x = a["L0_attn_x"]
    B, S, Dm = x.shape
    E = a["L0_ffn_router_w"].shape[1]
    rows = x.reshape(B * S, Dm)

    def bias_columns(b1):
        e, f = b1.shape
        return b1.reshape(e, f // P, P).transpose(2, 0, 1).reshape(P, -1)

    const_f, const_b = constants(B * S, E, B * S // P + E - 1)
    arrays = {
        "x_tok": rows, "x_t": rows.T,
        "wq0": a["L0_attn_Wq"], "wk0": a["L0_attn_Wk"], "wv0_t": a["L0_attn_Wv"].T,
        "router": a["L0_ffn_router_w"],
        "w1a": a["L0_ffn_w1"], "b1a": bias_columns(a["L0_ffn_b1"]), "w2a": a["L0_ffn_w2"], "b2a": a["L0_ffn_b2"],
        "wq1_t": a["L1_attn_Wq"].transpose(2, 1, 0), "wkv": a["L1_attn_Wkv_down"],
        "wku_t": a["L1_attn_Wk_up"].transpose(2, 1, 0), "wvu_t": a["L1_attn_Wv_up"].transpose(2, 1, 0),
        "wout": a["L1_attn_Wout"].transpose(1, 0, 2),
        "gate_w_t": a["L1_ffn_gate_w"].T, "gate_b": a["L1_ffn_gate_b"],
        "w1b": a["L1_ffn_w1"].transpose(0, 2, 1), "b1b": bias_columns(a["L1_ffn_b1"]),
        "w2b": a["L1_ffn_w2"].transpose(0, 2, 1), "b2b": a["L1_ffn_b2"],
        "const_f": const_f, "const_b": const_b,
    }
    nc = bacc.Bacc("TRN2", target_bir_lowering=False, num_devices=1)
    arrays = {f"in_{k}": np.ascontiguousarray(v) for k, v in arrays.items()}
    args = [nc.dram_tensor(k, v.shape, mybir.dt.from_np(v.dtype), kind="ExternalInput").ap() for k, v in arrays.items()]
    out = nc.dram_tensor("out_dram", (B * S, Dm), F32, kind="ExternalOutput").ap()
    build(nc, *args, out)
    r = run_bass_kernel_spmd(nc, [arrays], core_ids=[0])
    return r.results[0]["out_dram"].reshape(B, S, Dm)
```
